# Optimizing a Trainium2 kernel written in Bass

```python
import numpy as np
import jax
import jax.numpy as jnp

def _softmax(x, axis=-1):
    return jax.nn.softmax(x, axis=axis)

def _gelu(x):
    return jax.nn.gelu(x, approximate=True)

def _silu(x):
    return jax.nn.silu(x)

def _sigmoid(x):
    return jax.nn.sigmoid(x)

def _layernorm(x, axis=-1, eps=1e-05):
    m = jnp.mean(x, axis=axis, keepdims=True)
    v = jnp.var(x, axis=axis, keepdims=True)
    return (x - m) / jnp.sqrt(v + eps)

def _scatter_add(tgt, idx, src, axis=0):
    return tgt.at[idx].add(src)

def _segment_sum(src, seg, n):
    return jax.ops.segment_sum(src, seg, n)
kernel_name = 'mk_dlrm_tower_d1_rec_r8_ef8a60'

def setup_inputs(seed: int=0):
    np.random.seed(seed)
    _w = jnp.asarray

    def _rec_inputs():
        import jax
        import jax.numpy as jnp
        _tk = jax.random.key(seed)
        dense_ctx = jax.random.normal(jax.random.fold_in(_tk, 190), (2048, 16), jnp.float32)
        ids = jnp.stack([jax.random.randint(jax.random.fold_in(_tk, 200 + f), (2048,), 0, v, jnp.int32) for f, v in enumerate([125000, 12500, 12500, 1250, 1250, 125000, 12500, 12500, 1000, 125000, 12500, 12500, 1000, 1000, 1250, 12500, 1000, 12500, 1250, 1000, 1000, 1250, 1000, 1250, 1000, 1250, 1000, 1000, 1000, 1250, 1250, 1000])], axis=1)
        tbl_0 = 0.05 * jax.random.normal(jax.random.fold_in(_tk, 500 + 0), (125000, 64), jnp.float32)
        tbl_1 = 0.05 * jax.random.normal(jax.random.fold_in(_tk, 500 + 1), (12500, 64), jnp.float32)
        tbl_2 = 0.05 * jax.random.normal(jax.random.fold_in(_tk, 500 + 2), (12500, 64), jnp.float32)
        tbl_3 = 0.05 * jax.random.normal(jax.random.fold_in(_tk, 500 + 3), (1250, 64), jnp.float32)
        tbl_4 = 0.05 * jax.random.normal(jax.random.fold_in(_tk, 500 + 4), (1250, 64), jnp.float32)
        tbl_5 = 0.05 * jax.random.normal(jax.random.fold_in(_tk, 500 + 5), (125000, 64), jnp.float32)
        tbl_6 = 0.05 * jax.random.normal(jax.random.fold_in(_tk, 500 + 6), (12500, 64), jnp.float32)
        tbl_7 = 0.05 * jax.random.normal(jax.random.fold_in(_tk, 500 + 7), (12500, 64), jnp.float32)
        tbl_8 = 0.05 * jax.random.normal(jax.random.fold_in(_tk, 500 + 8), (1000, 64), jnp.float32)
        tbl_9 = 0.05 * jax.random.normal(jax.random.fold_in(_tk, 500 + 9), (125000, 64), jnp.float32)
        tbl_10 = 0.05 * jax.random.normal(jax.random.fold_in(_tk, 500 + 10), (12500, 64), jnp.float32)
        tbl_11 = 0.05 * jax.random.normal(jax.random.fold_in(_tk, 500 + 11), (12500, 64), jnp.float32)
        tbl_12 = 0.05 * jax.random.normal(jax.random.fold_in(_tk, 500 + 12), (1000, 64), jnp.float32)
        tbl_13 = 0.05 * jax.random.normal(jax.random.fold_in(_tk, 500 + 13), (1000, 64), jnp.float32)
        tbl_14 = 0.05 * jax.random.normal(jax.random.fold_in(_tk, 500 + 14), (1250, 64), jnp.float32)
        tbl_15 = 0.05 * jax.random.normal(jax.random.fold_in(_tk, 500 + 15), (12500, 64), jnp.float32)
        tbl_16 = 0.05 * jax.random.normal(jax.random.fold_in(_tk, 500 + 16), (1000, 64), jnp.float32)
        tbl_17 = 0.05 * jax.random.normal(jax.random.fold_in(_tk, 500 + 17), (12500, 64), jnp.float32)
        tbl_18 = 0.05 * jax.random.normal(jax.random.fold_in(_tk, 500 + 18), (1250, 64), jnp.float32)
        tbl_19 = 0.05 * jax.random.normal(jax.random.fold_in(_tk, 500 + 19), (1000, 64), jnp.float32)
        tbl_20 = 0.05 * jax.random.normal(jax.random.fold_in(_tk, 500 + 20), (1000, 64), jnp.float32)
        tbl_21 = 0.05 * jax.random.normal(jax.random.fold_in(_tk, 500 + 21), (1250, 64), jnp.float32)
        tbl_22 = 0.05 * jax.random.normal(jax.random.fold_in(_tk, 500 + 22), (1000, 64), jnp.float32)
        tbl_23 = 0.05 * jax.random.normal(jax.random.fold_in(_tk, 500 + 23), (1250, 64), jnp.float32)
        tbl_24 = 0.05 * jax.random.normal(jax.random.fold_in(_tk, 500 + 24), (1000, 64), jnp.float32)
        tbl_25 = 0.05 * jax.random.normal(jax.random.fold_in(_tk, 500 + 25), (1250, 64), jnp.float32)
        tbl_26 = 0.05 * jax.random.normal(jax.random.fold_in(_tk, 500 + 26), (1000, 64), jnp.float32)
        tbl_27 = 0.05 * jax.random.normal(jax.random.fold_in(_tk, 500 + 27), (1000, 64), jnp.float32)
        tbl_28 = 0.05 * jax.random.normal(jax.random.fold_in(_tk, 500 + 28), (1000, 64), jnp.float32)
        tbl_29 = 0.05 * jax.random.normal(jax.random.fold_in(_tk, 500 + 29), (1250, 64), jnp.float32)
        tbl_30 = 0.05 * jax.random.normal(jax.random.fold_in(_tk, 500 + 30), (1250, 64), jnp.float32)
        tbl_31 = 0.05 * jax.random.normal(jax.random.fold_in(_tk, 500 + 31), (1000, 64), jnp.float32)
        _rk = jax.random.fold_in(_tk, 7)
        W_top1 = 0.0441942 * jax.random.normal(jax.random.fold_in(_tk, 801), (512, 512), jnp.float32)
        W_top2 = 0.0441942 * jax.random.normal(jax.random.fold_in(_tk, 802), (512, 256), jnp.float32)
        W_top3 = 0.0625 * jax.random.normal(jax.random.fold_in(_tk, 803), (256, 1), jnp.float32)
        b_top1 = jnp.zeros((512,), jnp.float32)
        b_top2 = jnp.zeros((256,), jnp.float32)
        return (dense_ctx, ids, tbl_0, tbl_1, tbl_2, tbl_3, tbl_4, tbl_5, tbl_6, tbl_7, tbl_8, tbl_9, tbl_10, tbl_11, tbl_12, tbl_13, tbl_14, tbl_15, tbl_16, tbl_17, tbl_18, tbl_19, tbl_20, tbl_21, tbl_22, tbl_23, tbl_24, tbl_25, tbl_26, tbl_27, tbl_28, tbl_29, tbl_30, tbl_31, W_top1, b_top1, W_top2, b_top2, W_top3)
    dense_ctx, ids, tbl_0, tbl_1, tbl_2, tbl_3, tbl_4, tbl_5, tbl_6, tbl_7, tbl_8, tbl_9, tbl_10, tbl_11, tbl_12, tbl_13, tbl_14, tbl_15, tbl_16, tbl_17, tbl_18, tbl_19, tbl_20, tbl_21, tbl_22, tbl_23, tbl_24, tbl_25, tbl_26, tbl_27, tbl_28, tbl_29, tbl_30, tbl_31, W_top1, b_top1, W_top2, b_top2, W_top3 = _rec_inputs()

    def _L0_rec_setup():
        import jax, jax.numpy as jnp
        import numpy as np
        B, F, E = (512, 32, 64)
        P = F * (F - 1) // 2
        key = jax.random.key(seed)
        k1, k2 = jax.random.split(key)
        x = jax.random.normal(k1, (B, F, E), dtype=jnp.float32)
        kernel = jax.random.normal(k2, (E, P, E), dtype=jnp.float32) * 0.05
        return {'x': x, 'kernel': kernel}
    _L0_rec_all = _L0_rec_setup()
    _L0_rec_in = {k: v for k, v in _L0_rec_all.items() if k in ('kernel',)}
    del _L0_rec_all
    return {'dense_ctx': dense_ctx, 'ids': ids, 'tbl_0': tbl_0, 'tbl_1': tbl_1, 'tbl_2': tbl_2, 'tbl_3': tbl_3, 'tbl_4': tbl_4, 'tbl_5': tbl_5, 'tbl_6': tbl_6, 'tbl_7': tbl_7, 'tbl_8': tbl_8, 'tbl_9': tbl_9, 'tbl_10': tbl_10, 'tbl_11': tbl_11, 'tbl_12': tbl_12, 'tbl_13': tbl_13, 'tbl_14': tbl_14, 'tbl_15': tbl_15, 'tbl_16': tbl_16, 'tbl_17': tbl_17, 'tbl_18': tbl_18, 'tbl_19': tbl_19, 'tbl_20': tbl_20, 'tbl_21': tbl_21, 'tbl_22': tbl_22, 'tbl_23': tbl_23, 'tbl_24': tbl_24, 'tbl_25': tbl_25, 'tbl_26': tbl_26, 'tbl_27': tbl_27, 'tbl_28': tbl_28, 'tbl_29': tbl_29, 'tbl_30': tbl_30, 'tbl_31': tbl_31, 'W_top1': W_top1, 'b_top1': b_top1, 'W_top2': W_top2, 'b_top2': b_top2, 'W_top3': W_top3, 'L0_rec_kernel': _L0_rec_in['kernel']}

def reference(dense_ctx, ids, tbl_0, tbl_1, tbl_2, tbl_3, tbl_4, tbl_5, tbl_6, tbl_7, tbl_8, tbl_9, tbl_10, tbl_11, tbl_12, tbl_13, tbl_14, tbl_15, tbl_16, tbl_17, tbl_18, tbl_19, tbl_20, tbl_21, tbl_22, tbl_23, tbl_24, tbl_25, tbl_26, tbl_27, tbl_28, tbl_29, tbl_30, tbl_31, W_top1, b_top1, W_top2, b_top2, W_top3, L0_rec_kernel):
    import jax
    import jax.numpy as jnp

    def _L0_rec_ref(x, kernel):
        import jax, jax.numpy as jnp
        import numpy as np
        B, F, E = (512, 32, 64)
        P = F * (F - 1) // 2
        nf = x.shape[1]
        row_idx, col_idx = np.triu_indices(nf, k=1)
        p = x[:, row_idx, :]
        q = x[:, col_idx, :]
        kp = jnp.einsum('bpe,fpe,bpf->bp', p, kernel, q)
        return kp
    e = jnp.stack([tbl_0[ids[:, 0]], tbl_1[ids[:, 1]], tbl_2[ids[:, 2]], tbl_3[ids[:, 3]], tbl_4[ids[:, 4]], tbl_5[ids[:, 5]], tbl_6[ids[:, 6]], tbl_7[ids[:, 7]], tbl_8[ids[:, 8]], tbl_9[ids[:, 9]], tbl_10[ids[:, 10]], tbl_11[ids[:, 11]], tbl_12[ids[:, 12]], tbl_13[ids[:, 13]], tbl_14[ids[:, 14]], tbl_15[ids[:, 15]], tbl_16[ids[:, 16]], tbl_17[ids[:, 17]], tbl_18[ids[:, 18]], tbl_19[ids[:, 19]], tbl_20[ids[:, 20]], tbl_21[ids[:, 21]], tbl_22[ids[:, 22]], tbl_23[ids[:, 23]], tbl_24[ids[:, 24]], tbl_25[ids[:, 25]], tbl_26[ids[:, 26]], tbl_27[ids[:, 27]], tbl_28[ids[:, 28]], tbl_29[ids[:, 29]], tbl_30[ids[:, 30]], tbl_31[ids[:, 31]]], axis=1)
    z = _L0_rec_ref(e, L0_rec_kernel)
    z = z.reshape(z.shape[0], -1)
    h = jnp.concatenate([z, dense_ctx], axis=1)
    h = jnp.maximum(h @ W_top1 + b_top1, 0.0)
    h = jnp.maximum(h @ W_top2 + b_top2, 0.0)
    y = h @ W_top3
    return y

_drawn_inputs = setup_inputs


def setup_inputs(seed=0):
    import zlib

    import numpy as np

    out = dict(_drawn_inputs(seed))
    spreads = {'b_top1': (0.0, 0.1), 'b_top2': (0.0, 0.1)}
    factors = {'tbl_0': 6.413,
     'tbl_1': 5.931,
     'tbl_2': 5.79,
     'tbl_3': 5.841,
     'tbl_4': 4.74,
     'tbl_5': 6.029,
     'tbl_6': 5.631,
     'tbl_7': 5.011,
     'tbl_8': 5.646,
     'tbl_9': 5.807,
     'tbl_10': 5.564,
     'tbl_11': 5.427,
     'tbl_12': 5.258,
     'tbl_13': 5.173,
     'tbl_14': 5.735,
     'tbl_15': 5.652,
     'tbl_16': 5.334,
     'tbl_17': 5.952,
     'tbl_18': 5.013,
     'tbl_19': 5.405,
     'tbl_20': 5.226,
     'tbl_21': 5.622,
     'tbl_22': 5.976,
     'tbl_23': 5.897,
     'tbl_24': 5.938,
     'tbl_25': 5.478,
     'tbl_26': 5.614,
     'tbl_27': 5.534,
     'tbl_28': 5.855,
     'tbl_29': 5.589,
     'tbl_30': 5.66,
     'tbl_31': 6.04}
    for name, (base, spread) in spreads.items():
        noise = np.random.default_rng([zlib.crc32(name.encode()), seed]).standard_normal(out[name].shape)
        drawn = base * np.exp(spread * noise) if base else spread * noise
        out[name] = jnp.asarray(drawn.astype(out[name].dtype))
    for name, factor in factors.items():
        out[name] = (out[name] * factor).astype(out[name].dtype)
    return out
```

```python
from contextlib import ExitStack

import concourse.bass as bass
from concourse import mybir

F32 = mybir.dt.float32
F32R = mybir.dt.float32r
I32 = mybir.dt.int32
ALU = mybir.AluOpType
ACT = mybir.ActivationFunctionType

B, F, E = 2048, 32, 64
DENSE, H1, H2 = 16, 512, 256
P = 128
N = 512
CHUNKS = B // N
TILES = N // P

LEFT = F // 4
X_SLOTS = F // 2 - 1
L_SLOTS = 2


def group_list():
    groups = []
    for j in range(2, F):
        if j % 4 == 3:
            groups.append(("left", j, j // 4))
        groups += [("pair", j, k) for k in range(j // 2)]
    return groups


def slot_of(group):
    kind, _, k = group
    return k if kind == "pair" else X_SLOTS + k % L_SLOTS


def field_pairs(group):
    kind, j, k = group
    if kind == "pair":
        return (2 * k, j), (2 * k + 1, j)
    return (4 * k, 4 * k + 1), (4 * k + 2, 4 * k + 3)


def moving_fields(group):
    kind, j, k = group
    return (j,) if kind == "pair" else (4 * k + 1, 4 * k + 3)


GROUPS = group_list()
DUOS = len(GROUPS) // 2
QUADS = len(GROUPS) // 4
DUO = [sorted(GROUPS[2 * d:2 * d + 2], key=slot_of) for d in range(DUOS)]
REGULAR = [g for g in GROUPS if g[0] == "pair"]

Z_QUADS = P // 8
Z_BANKS = -(-QUADS // Z_QUADS)
SUM_ROWS = 2 * (QUADS - (Z_BANKS - 1) * Z_QUADS)

LEFT_COLS = LEFT * 3 * E
PIECE = 1024
PIECES = len(GROUPS) * 2 * E // PIECE
STAGES = 4
STAGE_SLOT = X_SLOTS - STAGES * PIECE // N
FIRST_STAGED_FIELD = 2 * STAGE_SLOT

ROWS_RING = 4
HALF_RING = 4


def kernel_piece(group):
    return 0 if group[0] == "left" else 1 + REGULAR.index(group) * 2 * E // PIECE


def duos_where(test):
    return [d for d in range(DUOS) if any(test(g) for g in DUO[d])]


FIRST_DUO = {j: duos_where(lambda g: j in (g[1],))[0] for j in range(2, F)}
LAST_MOVING = {j: duos_where(lambda g: j in moving_fields(g))[-1] for j in range(1, F)}
LAST_READ = {s: duos_where(lambda g: g[0] == "pair" and slot_of(g) == s)[-1] for s in range(X_SLOTS)}
LEFT_DUO = {m: duos_where(lambda g: g[0] == "left" and g[2] == m)[0] for m in range(LEFT)}
PIECES_BY = {j: min(PIECES, -(-PIECES * (j + 1) // (FIRST_STAGED_FIELD - 2))) for j in range(F)}
COPY_BEFORE = {kb: DUO[2 * (Z_QUADS * (kb + 1) + 1)][-1][1] + 3 for kb in range(Z_BANKS - 1)}


def z_rows():
    rows, dense = [], 0
    for kb in range(Z_BANKS):
        for r in range(P):
            column_tile, s, half = r // 32, r % 32 // 2, r % 2
            quad = kb * Z_QUADS + s
            if quad < QUADS:
                group = DUO[2 * quad + column_tile // 2][column_tile % 2]
                rows.append(field_pairs(group)[half])
            else:
                rows.append(dense)
                dense += 1
    return rows


def dlrm_tower(nc, ids, tables, pair_kernel, dense, w1, b1, w2, b2, w3, z_dram, out):
    with ExitStack() as ctx:
        def psum(name, shape):
            return ctx.enter_context(nc.psum_tensor(name, shape, F32))

        def sem(name):
            return ctx.enter_context(nc.semaphore(name))

        place = [-(-nc.sbuf_base // 32) * 32]

        def sb(name, shape, dt, at=place):
            width = 4
            for s in shape[1:]:
                width *= s
            t = nc.alloc_sbuf_tensor_at(name, shape, dt, offset=at[0])
            at[0] += -(-width // 32) * 32
            return t

        kernel_at = place[0]
        k_left = sb("k_left", [P, LEFT, 3, E], F32R)
        freed = [place[0]]
        k_reg = sb("k_reg", [P, len(REGULAR), 2 * E], F32R)
        multiplier = sb("multiplier", [P, X_SLOTS + L_SLOTS, N], F32)
        rows = sb("rows", [P, ROWS_RING, TILES, 2, E], F32)
        halves = sb("halves", [P, HALF_RING, 2, N], F32R)
        products = sb("products", [P, 4, 2, N], F32)
        sums = sb("sums", [P, N], F32)
        idx = sb("idx", [P, TILES, F], I32)
        identity = sb("identity", [P, P], F32)
        selector = sb("selector", [P, 62], F32)
        w1_sb = sb("w1_sb", [P, 4, H1], F32, freed)
        w2_sb = sb("w2_sb", [P, 4, H2], F32, freed)
        w3_sb = sb("w3_sb", [P, 2], F32, freed)
        b1_sb = sb("b1_sb", [P, 4], F32, freed)
        b2_sb = sb("b2_sb", [P, 2], F32, freed)
        z_sb = sb("z_sb", [P, CHUNKS, Z_BANKS, N], F32, freed)
        h1_sb = sb("h1_sb", [P, 2, 4, N], F32, freed)
        h2_sb = sb("h2_sb", [P, 2, 2, N], F32, freed)
        y_sb = sb("y_sb", [1, B], F32, freed)
        freed_groups = -(-(freed[0] - kernel_at - 4 * LEFT_COLS) // (4 * 2 * E))
        freed_duo = FIRST_DUO[REGULAR[freed_groups][1] + 1]

        y_ps = [psum(f"y_ps{i}", [P, 2, N]) for i in range(2)]
        sum_ps = [psum(f"sum_ps{i}", [P, N]) for i in range(2)]
        turned = [psum(f"turned{i}", [P, N]) for i in range(2)]

        ids_landed = sem("ids_landed")
        rows_landed = [sem(f"rows_landed{i}") for i in range(ROWS_RING)]
        rows_doubled = sem("rows_doubled")
        pool_passed = sem("pool_passed")
        identity_cleared = sem("identity_cleared")
        identity_made = sem("identity_made")
        selector_cleared = sem("selector_cleared")
        selector_made = sem("selector_made")
        zeros_made = sem("zeros_made")
        kernel_landed = [sem(f"kernel_landed{i}") for i in range(STAGES)]
        kernel_high = sem("kernel_high")
        kernel_split = sem("kernel_split")
        field_turned = sem("field_turned")
        field_stored = sem("field_stored")
        field_split = sem("field_split")
        duo_ready = sem("duo_ready")
        duo_multiplied = sem("duo_multiplied")
        quad_summed = sem("quad_summed")
        bank_copied = sem("bank_copied")
        bank_spilled = sem("bank_spilled")
        dense_placed = sem("dense_placed")
        weights_landed = sem("weights_landed")
        z_landed = [sem(f"z_landed{c}") for c in range(CHUNKS)]
        h1_ready = sem("h1_ready")
        h1_kept = sem("h1_kept")
        h2_ready = sem("h2_ready")
        h2_kept = sem("h2_kept")
        y_ready = sem("y_ready")
        y_kept = sem("y_kept")
        out_written = sem("out_written")

        SPILLED = (Z_BANKS - 1 + 4) * 16
        block = ctx.enter_context(nc.Block())

        @block.gpsimd
        def _(pool):
            nc.gpsimd.memset(identity[:], 0.0).then_inc(identity_cleared, 1)
            pool.wait_ge(identity_cleared, 1)
            nc.gpsimd.affine_select(out=identity[:], in_=identity[:], compare_op=ALU.not_equal, fill=1.0, base=0,
                                    pattern=[[-1, P]], channel_multiplier=1).then_inc(identity_made, 1)

            def double(c, j):
                s = j % ROWS_RING
                pool.wait_ge(rows_landed[s], (c * (F // ROWS_RING) + j // ROWS_RING + 1) * TILES * 16)
                pool.sem_inc(pool_passed, 1)
                nc.gpsimd.tensor_copy(rows[:, s, :, 1, :], rows[:, s, :, 0, :]).then_inc(rows_doubled, 1)

            def gather(c, first):
                src = ids[:, 0] if first else ids[:, bass.ds(c, 1)].rearrange("p o t f -> p (o t) f")
                pool.dma_start(idx[:], src).then_inc(ids_landed, 16)
                pool.wait_ge(ids_landed, c * 16 + 16)
                pool.sem_inc(pool_passed, 1)
                for j in range(F):
                    if not first or j >= ROWS_RING:
                        pool.wait_ge(field_turned, c * F + (j - ROWS_RING + 1))
                        pool.sem_inc(pool_passed, 1)
                    for t in range(TILES):
                        pool.indirect_dma_start(rows[:, j % ROWS_RING, t, 0, :], None, tables[j],
                                                bass.IndirectOffsetOnAxis(ap=idx[:, t, j:j + 1], axis=0)
                                                ).then_inc(rows_landed[j % ROWS_RING], 16)
                    if j:
                        double(c, j - 1)
                double(c, F - 1)

            gather(0, True)
            with pool.Fori(1, CHUNKS) as c:
                gather(c, False)

        @block.sync
        def _(sp):
            for p in range(PIECES):
                if p >= STAGES:
                    sp.wait_ge(kernel_split, p - STAGES + 1)
                at = STAGE_SLOT + 2 * (p % STAGES)
                for half in range(2):
                    sp.dma_start(multiplier[half * E:half * E + E, at:at + 2, :],
                                 pair_kernel[p].rearrange("f (s n) -> f s n", s=2)).then_inc(kernel_landed[p % STAGES], 16)
            for q in range(4):
                sp.dma_start(z_dram[Z_BANKS - 1, q * 32 + SUM_ROWS:q * 32 + 32, :],
                             dense[q * 4:q * 4 + 4, :]).then_inc(dense_placed, 16)

            def spill(c, kb):
                sp.wait_ge(bank_copied, c * Z_BANKS + kb + 1)
                if kb < Z_BANKS - 1:
                    sp.dma_start(z_dram[kb, :, bass.ds(c * N, N)], sums[:]).then_inc(bank_spilled, 16)
                else:
                    for q in range(4):
                        sp.dma_start(z_dram[kb, q * 32:q * 32 + SUM_ROWS, bass.ds(c * N, N)],
                                     sums[q * 32:q * 32 + SUM_ROWS, :]).then_inc(bank_spilled, 16)

            for kb in range(Z_BANKS - 1):
                spill(0, kb)
            with sp.Fori(1, CHUNKS) as c:
                spill(c - 1, Z_BANKS - 1)
                for kb in range(Z_BANKS - 1):
                    spill(c, kb)

            sp.wait_ge(duo_ready, (CHUNKS - 1) * DUOS + freed_duo)
            for dst, src in ((w1_sb, w1), (w2_sb, w2), (w3_sb, w3), (b1_sb, b1), (b2_sb, b2)):
                sp.dma_start(dst[:], src).then_inc(weights_landed, 16)
            sp.wait_ge(dense_placed, 4 * 16)
            for c in range(CHUNKS):
                if c == CHUNKS - 1:
                    spill(c, Z_BANKS - 1)
                sp.wait_ge(bank_spilled, (c + 1) * SPILLED)
                sp.dma_start(z_sb[:, c], z_dram[:, :, c * N:c * N + N].rearrange("k p n -> p k n")).then_inc(z_landed[c], 16)
            sp.wait_ge(y_kept, CHUNKS)
            sp.dma_start(out, y_sb[:]).then_inc(out_written, 16)
            sp.wait_ge(out_written, 16)

        @block.tensor
        def _(pe):
            def turn(c, j, first):
                pe.wait_ge(rows_doubled, c * F + j + 1)
                if j == 2:
                    pe.wait_ge(field_stored, c * F + 1)
                elif j > 2:
                    pe.wait_ge(field_split, c * (F - 1) + j - 2)
                elif not first:
                    pe.wait_ge(field_split, c * (F - 1) + j - 1)
                for t in range(TILES):
                    last = nc.tensor.transpose(turned[j % 2][:, t * P:(t + 1) * P],
                                               rows[:, j % ROWS_RING, t].rearrange("p d e -> p (d e)"),
                                               identity[:])
                last.then_inc(field_turned, 1)

            def bilinear(c, d, first):
                if not first or d >= 2:
                    pe.wait_ge(duo_multiplied, c * DUOS + d - 1)
                for bank, group in enumerate(DUO[d]):
                    kind, j, k = group
                    if kind == "pair":
                        r = REGULAR.index(group)
                        parts = [(k_reg[:, r, :], j)]
                    else:
                        blocks = k_left[:, k].rearrange("p b e -> p (b e)")
                        parts = [(blocks[:, 0:2 * E], 4 * k + 1), (blocks[:, E:3 * E], 4 * k + 3)]
                    for n, (stationary, field) in enumerate(parts):
                        for half in range(2):
                            last = nc.tensor.matmul(y_ps[d % 2][:, bank, :], stationary,
                                                    halves[:, field % HALF_RING, half, :],
                                                    start=(n == 0 and half == 0),
                                                    stop=(n == len(parts) - 1 and half == 1))
                last.then_inc(duo_ready, 1)

            def add_up(c, quad, first):
                pe.wait_ge(duo_multiplied, c * DUOS + 2 * quad + 2)
                kb, s = quad // Z_QUADS, quad % Z_QUADS
                if s == 0 and not (first and kb < 2):
                    pe.wait_ge(bank_copied, c * Z_BANKS + kb - 1)
                for q in range(4):
                    last = nc.tensor.matmul(sum_ps[kb % 2][32 * q:32 * q + 32, :], selector[:, 30 - 2 * s:62 - 2 * s],
                                            products[:, (2 * quad + q // 2) % 4, q % 2, :],
                                            start=(s == 0), stop=(s == Z_QUADS - 1 or quad == QUADS - 1))
                last.then_inc(quad_summed, 1)

            def chunk(c, first):
                if first:
                    pe.wait_ge(identity_made, 1)
                    turn(c, 0, first)
                    turn(c, 1, first)
                turn(c, 2, first)
                if first:
                    pe.wait_ge(zeros_made, 1)
                    pe.wait_ge(selector_made, 2)
                else:
                    add_up(c - 1, QUADS - 1, False)
                turn(c, 3, first)
                pieces = 0
                for d in range(DUOS):
                    for j in range(2, F):
                        if FIRST_DUO[j] == d:
                            if j + 2 < F:
                                turn(c, j + 2, first)
                            elif first:
                                turn(c + 1, j + 2 - F, False)
                            else:
                                with pe.If(c < CHUNKS - 1):
                                    turn(c + 1, j + 2 - F, False)
                            pe.wait_ge(field_split, c * (F - 1) + j)
                    if first and max(map(kernel_piece, DUO[d])) + 1 > pieces:
                        pieces = max(map(kernel_piece, DUO[d])) + 1
                        pe.wait_ge(kernel_split, pieces)
                    bilinear(c, d, first)
                    if d % 2 and d > 2:
                        add_up(c, d // 2 - 1, first)

            chunk(0, True)
            with pe.Fori(1, CHUNKS) as c:
                chunk(c, False)
            add_up(CHUNKS - 1, QUADS - 1, False)

            def layer1(c):
                pe.wait_ge(z_landed[c], 16)
                for n in range(4):
                    if c:
                        pe.wait_ge(h1_kept, (c - 1) * 4 + n + 1)
                    else:
                        pe.wait_ge(duo_multiplied, CHUNKS * DUOS)
                    for kb in range(4):
                        last = nc.tensor.matmul(y_ps[n // 2][:, n % 2, :], w1_sb[:, kb, n * P:n * P + P],
                                                z_sb[:, c, kb, :], start=(kb == 0), stop=(kb == 3))
                    last.then_inc(h1_ready, 1)

            def layer2(c):
                pe.wait_ge(h1_kept, 4 * c + 4)
                for n in range(2):
                    if c:
                        pe.wait_ge(h2_kept, (c - 1) * 2 + n + 1)
                    else:
                        pe.wait_ge(bank_copied, CHUNKS * Z_BANKS)
                    for kb in range(4):
                        last = nc.tensor.matmul(sum_ps[n][:], w2_sb[:, kb, n * P:n * P + P], h1_sb[:, c % 2, kb, :],
                                                start=(kb == 0), stop=(kb == 3))
                    last.then_inc(h2_ready, 1)

            def layer3(c):
                pe.wait_ge(h2_kept, 2 * c + 2)
                if c >= 2:
                    pe.wait_ge(y_kept, c - 1)
                for kb in range(2):
                    last = nc.tensor.matmul(turned[c % 2][0:1, :], w3_sb[:, kb:kb + 1], h2_sb[:, c % 2, kb, :],
                                            start=(kb == 0), stop=(kb == 1))
                last.then_inc(y_ready, 1)

            pe.wait_ge(weights_landed, 5 * 16)
            for step in range(CHUNKS + 2):
                if step < CHUNKS:
                    layer1(step)
                if 1 <= step <= CHUNKS:
                    layer2(step - 1)
                if step >= 2:
                    layer3(step - 2)

        @block.scalar
        def _(act):
            def kernel_piece_high(p):
                act.wait_ge(kernel_landed[p % STAGES], (p // STAGES + 1) * 32)
                at = STAGE_SLOT + 2 * (p % STAGES)
                staged = multiplier[:, at:at + 2, :]
                if p == 0:
                    dst = k_left[:, :, 0:3:2, :]
                    staged = staged.rearrange("p s n -> p (s n)").rearrange("p (m b e) -> p m b e", b=2, e=E)
                else:
                    dst = k_reg[:, (p - 1) * 8:p * 8, :]
                    staged = staged.rearrange("p s n -> p (s n)").rearrange("p (g n) -> p g n", g=8)
                nc.scalar.activation(dst, staged, ACT.Copy).then_inc(kernel_high, 1)

            def store(c, j, first):
                act.wait_ge(field_turned, c * F + j + 1)
                bank = turned[j % 2]
                ops = []
                if j:
                    if j > HALF_RING:
                        act.wait_ge(duo_ready, c * DUOS + LAST_MOVING[j - HALF_RING] + 1)
                    elif not first:
                        before = j + F - HALF_RING if j < HALF_RING else F - HALF_RING
                        act.wait_ge(duo_ready, (c - 1) * DUOS + LAST_MOVING[before] + 1)
                    last = nc.scalar.activation(halves[:, j % HALF_RING, 0, :], bank[:], ACT.Copy)
                if j < 2 * X_SLOTS:
                    if not first:
                        act.wait_ge(duo_multiplied, (c - 1) * DUOS + LAST_READ[j // 2] + 1)
                    elif j == FIRST_STAGED_FIELD:
                        act.wait_ge(kernel_split, PIECES)
                    at = j % 2 * E
                    last = nc.scalar.activation(multiplier[at:at + E, j // 2, :], bank[at:at + E, :], ACT.Copy)
                if j % 2 == 0:
                    m = j // 4
                    if m >= L_SLOTS:
                        act.wait_ge(duo_multiplied, c * DUOS + LEFT_DUO[m - L_SLOTS] + 1)
                    elif not first:
                        act.wait_ge(duo_multiplied, (c - 1) * DUOS + LEFT_DUO[m - L_SLOTS + LEFT] + 1)
                    at = j % 4 // 2 * E
                    last = nc.scalar.activation(multiplier[at:at + E, X_SLOTS + m % L_SLOTS, :], bank[at:at + E, :], ACT.Copy)
                last.then_inc(field_stored, 1)

            def copy_bank(c, kb, first):
                act.wait_ge(quad_summed, c * QUADS + min(Z_QUADS * (kb + 1), QUADS))
                if not first or kb:
                    act.wait_ge(bank_spilled, c * SPILLED + kb * 16)
                nc.scalar.activation(sums[:], sum_ps[kb % 2][:], ACT.Copy).then_inc(bank_copied, 1)

            def chunk(c, first):
                for j in range(F):
                    if first:
                        for p in range(PIECES_BY[j - 1] if j else 0, PIECES_BY[j]):
                            kernel_piece_high(p)
                    for kb in range(Z_BANKS - 1):
                        if COPY_BEFORE[kb] == j:
                            copy_bank(c, kb, first)
                    store(c, j, first)
                    if j == 2 and not first:
                        copy_bank(c - 1, Z_BANKS - 1, False)
                for kb in range(Z_BANKS - 1):
                    if COPY_BEFORE[kb] >= F:
                        copy_bank(c, kb, first)

            chunk(0, True)
            with act.Fori(1, CHUNKS) as c:
                chunk(c, False)
            copy_bank(CHUNKS - 1, Z_BANKS - 1, False)

            def keep1(c):
                if c >= 2:
                    act.wait_ge(h2_ready, 2 * (c - 1))
                for n in range(4):
                    act.wait_ge(h1_ready, 4 * c + n + 1)
                    nc.scalar.activation(h1_sb[:, c % 2, n, :], y_ps[n // 2][:, n % 2, :], ACT.Relu,
                                         bias=b1_sb[:, n:n + 1]).then_inc(h1_kept, 1)

            def keep2(c):
                if c >= 2:
                    act.wait_ge(y_ready, c - 1)
                for n in range(2):
                    act.wait_ge(h2_ready, 2 * c + n + 1)
                    nc.scalar.activation(h2_sb[:, c % 2, n, :], sum_ps[n][:], ACT.Relu,
                                         bias=b2_sb[:, n:n + 1]).then_inc(h2_kept, 1)

            act.wait_ge(weights_landed, 5 * 16)
            for step in range(CHUNKS + 1):
                if step < CHUNKS:
                    keep1(step)
                if step >= 1:
                    keep2(step - 1)

        @block.vector
        def _(dve):
            nc.vector.memset(k_left[:, :, 1, :].bitcast(F32), 0.0).then_inc(zeros_made, 1)
            nc.vector.memset(selector[:], 0.0).then_inc(selector_cleared, 1)
            dve.wait_ge(selector_cleared, 1)
            nc.vector.memset(selector[0:E, 30:31], 1.0).then_inc(selector_made, 1)
            nc.vector.memset(selector[E:P, 31:32], 1.0).then_inc(selector_made, 1)

            def kernel_piece_low(p):
                dve.wait_ge(kernel_high, p + 1)
                at = STAGE_SLOT + 2 * (p % STAGES)
                staged = multiplier[E:P, at:at + 2, :]
                if p == 0:
                    dst = k_left[E:P, :, 0:3:2, :]
                    staged = staged.rearrange("p s n -> p (s n)").rearrange("p (m b e) -> p m b e", b=2, e=E)
                else:
                    dst = k_reg[E:P, (p - 1) * 8:p * 8, :]
                    staged = staged.rearrange("p s n -> p (s n)").rearrange("p (g n) -> p g n", g=8)
                nc.vector.tensor_tensor(dst, staged, dst.bitcast(F32), ALU.subtract).then_inc(kernel_split, 1)

            def split(c, j):
                dve.wait_ge(field_stored, c * F + j + 1)
                nc.vector.tensor_tensor(halves[:, j % HALF_RING, 1, :], turned[j % 2][:],
                                        halves[:, j % HALF_RING, 0, :].bitcast(F32), ALU.subtract).then_inc(field_split, 1)

            def multiply(c, d, first):
                if not first or d >= 4:
                    dve.wait_ge(quad_summed, c * QUADS + d // 2 - 1)
                dve.wait_ge(duo_ready, c * DUOS + d + 1)
                s0, s1 = (slot_of(g) for g in DUO[d])
                if s0 == s1:
                    for bank in range(2):
                        last = nc.vector.tensor_tensor(products[:, d % 4, bank, :], y_ps[d % 2][:, bank, :],
                                                       multiplier[:, s0, :], ALU.mult)
                else:
                    last = nc.vector.tensor_tensor(products[:, d % 4], y_ps[d % 2][:],
                                                   multiplier[:, s0:s1 + 1:s1 - s0, :], ALU.mult)
                last.then_inc(duo_multiplied, 1)

            def chunk(c, first):
                def split_next(j):
                    if first:
                        for p in range(PIECES_BY[j - 1] if j > 1 else 0, PIECES_BY[j]):
                            kernel_piece_low(p)
                    split(c, j)

                for j in range(1, 4):
                    split_next(j)
                for d in range(DUOS):
                    for j in range(4, F):
                        if min(FIRST_DUO[j - 2] + 2, FIRST_DUO[j]) == d:
                            split_next(j)
                    for j in range(2, F):
                        if FIRST_DUO[j] == d:
                            dve.wait_ge(field_stored, c * F + j)
                    multiply(c, d, first)

            chunk(0, True)
            with dve.Fori(1, CHUNKS) as c:
                chunk(c, False)

            for c in range(CHUNKS):
                dve.wait_ge(y_ready, c + 1)
                nc.vector.tensor_copy(y_sb[:, c * N:c * N + N], turned[c % 2][0:1, :]).then_inc(y_kept, 1)


def kernel(**inputs):
    import numpy as np
    import concourse.bacc as bacc
    from concourse.bass_utils import run_bass_kernel_spmd

    pair_number = {}
    for i in range(F):
        for j in range(i + 1, F):
            pair_number[i, j] = len(pair_number)

    ids = np.ascontiguousarray(np.asarray(inputs["ids"]).reshape(CHUNKS, TILES, P, F).transpose(2, 0, 1, 3))
    order = [pair_number[p] for g in sorted(GROUPS, key=lambda g: g[0] != "left") for p in field_pairs(g)]
    k = np.asarray(inputs["L0_rec_kernel"])[:, order, :].reshape(E, PIECES, PIECE)
    pair_kernel = np.ascontiguousarray(k.transpose(1, 0, 2))
    pairs = len(pair_number)
    w1_rows = [pair_number[r] if isinstance(r, tuple) else pairs + r for r in z_rows()]
    w1 = np.ascontiguousarray(np.asarray(inputs["W_top1"])[w1_rows].reshape(4, P, H1).transpose(1, 0, 2))
    w2 = np.ascontiguousarray(np.asarray(inputs["W_top2"]).reshape(4, P, H2).transpose(1, 0, 2))
    w3 = np.ascontiguousarray(np.asarray(inputs["W_top3"]).reshape(2, P).T)
    b1 = np.ascontiguousarray(np.asarray(inputs["b_top1"]).reshape(4, P).T)
    b2 = np.ascontiguousarray(np.asarray(inputs["b_top2"]).reshape(2, P).T)
    dense = np.ascontiguousarray(np.asarray(inputs["dense_ctx"]).T)

    arrays = {"ids": ids, "pair_kernel": pair_kernel, "dense": dense, "w1": w1, "b1": b1, "w2": w2, "b2": b2, "w3": w3}
    for f in range(F):
        arrays[f"tbl_{f}"] = np.ascontiguousarray(inputs[f"tbl_{f}"])

    nc = bacc.Bacc("TRN2", target_bir_lowering=False, num_devices=1)
    ap = {n: nc.dram_tensor(n + "_dram", a.shape, mybir.dt.from_np(a.dtype), kind="ExternalInput").ap()
          for n, a in arrays.items()}
    z_dram = nc.dram_tensor("z_dram", (Z_BANKS, P, B), F32, kind="Internal").ap()
    out = nc.dram_tensor("out_dram", (1, B), F32, kind="ExternalOutput").ap()
    dlrm_tower(nc, ap["ids"], [ap[f"tbl_{f}"] for f in range(F)], ap["pair_kernel"], ap["dense"], ap["w1"], ap["b1"],
               ap["w2"], ap["b2"], ap["w3"], z_dram, out)
    r = run_bass_kernel_spmd(nc, [{n + "_dram": a for n, a in arrays.items()}], core_ids=[0])
    return r.results[0]["out_dram"].reshape(B, 1)
```

```python
from contextlib import ExitStack

import concourse.bass as bass
from concourse import mybir

F32 = mybir.dt.float32
F32R = mybir.dt.float32r
I32 = mybir.dt.int32
ALU = mybir.AluOpType
ACT = mybir.ActivationFunctionType

B, F, E = 2048, 32, 64
DENSE, H1, H2 = 16, 512, 256
P = 128
N = 512
CHUNKS = B // N
TILES = N // P

LEFT = F // 4
X_SLOTS = F // 2 - 1
L_SLOT = X_SLOTS


def group_list():
    groups = []
    for j in range(2, F):
        if j % 4 == 3:
            groups.append(("left", j, j // 4))
        groups += [("pair", j, k) for k in range(j // 2)]
    return groups


def slot_of(group):
    kind, _, k = group
    return k if kind == "pair" else L_SLOT


def field_pairs(group):
    kind, j, k = group
    if kind == "pair":
        return (2 * k, j), (2 * k + 1, j)
    return (4 * k, 4 * k + 1), (4 * k + 2, 4 * k + 3)


def moving_fields(group):
    kind, j, k = group
    return (j,) if kind == "pair" else (4 * k + 1, 4 * k + 3)


GROUPS = group_list()
DUOS = len(GROUPS) // 2
QUADS = len(GROUPS) // 4
DUO = [sorted(GROUPS[2 * d:2 * d + 2], key=slot_of) for d in range(DUOS)]
REGULAR = [g for g in GROUPS if g[0] == "pair"]

Z_QUADS = P // 8
Z_BANKS = -(-QUADS // Z_QUADS)
SUM_ROWS = 2 * (QUADS - (Z_BANKS - 1) * Z_QUADS)

LEFT_COLS = LEFT * 3 * E
PIECE = 1024
PIECES = len(GROUPS) * 2 * E // PIECE
STAGES, LATE_STAGES = 4, 2
EARLY = PIECES - STAGES
BORROWED_SLOT = X_SLOTS - LATE_STAGES * PIECE // N
FIRST_BORROWED_FIELD = 2 * BORROWED_SLOT

ROWS_RING = 8
HALF_RING = 4


def stage_of(p):
    if p < EARLY:
        return p % STAGES, p // STAGES + 1
    return STAGES + (p - EARLY) % LATE_STAGES, (p - EARLY) // LATE_STAGES + 1


def kernel_piece(group):
    return 0 if group[0] == "left" else 1 + REGULAR.index(group) * 2 * E // PIECE


def duos_where(test):
    return [d for d in range(DUOS) if any(test(g) for g in DUO[d])]


FIRST_DUO = {j: duos_where(lambda g: j in (g[1],))[0] for j in range(2, F)}
LAST_MOVING = {j: duos_where(lambda g: j in moving_fields(g))[-1] for j in range(1, F)}
LAST_READ = {s: duos_where(lambda g: g[0] == "pair" and slot_of(g) == s)[-1] for s in range(X_SLOTS)}
LEFT_DUO = {m: duos_where(lambda g: g[0] == "left" and g[2] == m)[0] for m in range(LEFT)}
PIECES_BY = {j: min(PIECES, -(-PIECES * (j + 1) // (FIRST_BORROWED_FIELD - 2))) for j in range(F)}
NEXT_TURN = {FIRST_DUO[F - 2]: 0, FIRST_DUO[F - 1]: 1, FIRST_DUO[F - 1] + 4: 2, FIRST_DUO[F - 1] + 6: 3}
NEXT_SPLIT = {FIRST_DUO[F - 1] // 2 * 2 + 6: 1}


def split_before():
    at = {}
    for j in range(4, F):
        early, late = FIRST_DUO[j - 2] + 2, FIRST_DUO[j]
        at[j] = min(early - 1, late) if j < 10 else early + early % 2 if early + early % 2 <= late else min(early, late)
    return at


SPLIT_BEFORE = split_before()
COPY_BEFORE = {kb: DUO[2 * (Z_QUADS * (kb + 1) + 1)][-1][1] + 3 for kb in range(Z_BANKS - 1)}


def z_rows():
    rows, dense = [], 0
    for kb in range(Z_BANKS):
        for r in range(P):
            column_tile, s, half = r // 32, r % 32 // 2, r % 2
            quad = kb * Z_QUADS + s
            if quad < QUADS:
                group = DUO[2 * quad + column_tile // 2][column_tile % 2]
                rows.append(field_pairs(group)[half])
            else:
                rows.append(dense)
                dense += 1
    return rows


def dlrm_tower(nc, ids, tables, pair_kernel, dense, w1, b1, w2, b2, w3, z_dram, out):
    with ExitStack() as ctx:
        def psum(name, shape):
            return ctx.enter_context(nc.psum_tensor(name, shape, F32))

        def sem(name):
            return ctx.enter_context(nc.semaphore(name))

        place = [-(-nc.sbuf_base // 32) * 32]

        def sb(name, shape, dt, at=place):
            width = 4
            for s in shape[1:]:
                width *= s
            t = nc.alloc_sbuf_tensor_at(name, shape, dt, offset=at[0])
            at[0] += -(-width // 32) * 32
            return t

        kernel_at = place[0]
        k_left = sb("k_left", [P, LEFT, 3, E], F32R)
        freed = [place[0]]
        k_reg = sb("k_reg", [P, len(REGULAR), 2 * E], F32R)
        staged = [nc.alloc_sbuf_tensor_at(f"staged{i}", [P, PIECE], F32,
                                          offset=freed[0] + (EARLY - 1 + i) * 4 * PIECE) for i in range(STAGES)]
        multiplier = sb("multiplier", [P, X_SLOTS + 1, N], F32)
        rows = sb("rows", [P, ROWS_RING, TILES, E], F32)
        doubled = sb("doubled", [P, TILES, 2, E], F32)
        halves = sb("halves", [P, HALF_RING, 2, N], F32R)
        products = sb("products", [P, 4, 2, N], F32)
        sums = sb("sums", [P, N], F32)
        idx = sb("idx", [P, TILES, F], I32)
        identity = sb("identity", [P, P], F32)
        selector = sb("selector", [P, 62], F32)
        w1_sb = sb("w1_sb", [P, 4, H1], F32, freed)
        w2_sb = sb("w2_sb", [P, 4, H2], F32, freed)
        w3_sb = sb("w3_sb", [P, 2], F32, freed)
        b1_sb = sb("b1_sb", [P, 4], F32, freed)
        b2_sb = sb("b2_sb", [P, 2], F32, freed)
        z_sb = sb("z_sb", [P, CHUNKS, Z_BANKS, N], F32, freed)
        h1_sb = sb("h1_sb", [P, 2, 4, N], F32, freed)
        h2_sb = sb("h2_sb", [P, 2, 2, N], F32, freed)
        y_sb = sb("y_sb", [1, B], F32, freed)
        freed_groups = -(-(freed[0] - kernel_at - 4 * LEFT_COLS) // (4 * 2 * E))
        freed_duo = FIRST_DUO[REGULAR[freed_groups][1] + 1]

        y_ps = [psum(f"y_ps{i}", [P, 2, N]) for i in range(2)]
        sum_ps = [psum(f"sum_ps{i}", [P, N]) for i in range(2)]
        turned = [psum(f"turned{i}", [P, N]) for i in range(2)]

        ids_landed = sem("ids_landed")
        rows_landed = [sem(f"rows_landed{i}") for i in range(ROWS_RING)]
        rows_doubled = sem("rows_doubled")
        pool_passed = sem("pool_passed")
        identity_cleared = sem("identity_cleared")
        identity_made = sem("identity_made")
        selector_cleared = sem("selector_cleared")
        selector_made = sem("selector_made")
        zeros_made = sem("zeros_made")
        kernel_landed = [sem(f"kernel_landed{i}") for i in range(STAGES + LATE_STAGES)]
        kernel_high = sem("kernel_high")
        kernel_split = sem("kernel_split")
        field_turned = sem("field_turned")
        field_stored = sem("field_stored")
        field_split = sem("field_split")
        duo_ready = sem("duo_ready")
        duo_multiplied = sem("duo_multiplied")
        quad_summed = sem("quad_summed")
        bank_copied = sem("bank_copied")
        bank_spilled = sem("bank_spilled")
        dense_placed = sem("dense_placed")
        weights_landed = sem("weights_landed")
        z_landed = [sem(f"z_landed{c}") for c in range(CHUNKS)]
        h1_ready = sem("h1_ready")
        h1_kept = sem("h1_kept")
        h2_ready = sem("h2_ready")
        h2_kept = sem("h2_kept")
        y_ready = sem("y_ready")
        y_kept = sem("y_kept")
        out_written = sem("out_written")

        SPILLED = (Z_BANKS - 1 + 4) * 16

        def loaded(p, lo, hi):
            stage = stage_of(p)[0]
            if stage < STAGES:
                return staged[stage][lo:hi, :]
            at = BORROWED_SLOT + (stage - STAGES) * PIECE // N
            return multiplier[lo:hi, at:at + PIECE // N, :].rearrange("p s n -> p (s n)")

        def kept(p, lo, hi):
            if p == 0:
                return k_left[lo:hi, :, 0:3:2, :]
            return k_reg[lo:hi, (p - 1) * 8:p * 8, :].rearrange("p g (b e) -> p g b e", e=E)

        block = ctx.enter_context(nc.Block())

        @block.gpsimd
        def _(pool):
            nc.gpsimd.memset(identity[:], 0.0).then_inc(identity_cleared, 1)
            pool.wait_ge(identity_cleared, 1)
            nc.gpsimd.affine_select(out=identity[:], in_=identity[:], compare_op=ALU.not_equal, fill=1.0, base=0,
                                    pattern=[[-1, P]], channel_multiplier=1).then_inc(identity_made, 1)

            def gather(c, first):
                if not first:
                    for s in range(ROWS_RING):
                        pool.wait_ge(rows_landed[s], c * (F // ROWS_RING) * TILES * 16)
                        pool.sem_inc(pool_passed, 1)
                src = ids[:, 0] if first else ids[:, bass.ds(c, 1)].rearrange("p o t f -> p (o t) f")
                pool.dma_start(idx[:], src).then_inc(ids_landed, 16)
                pool.wait_ge(ids_landed, c * 16 + 16)
                pool.sem_inc(pool_passed, 1)
                for j in range(F):
                    if not first or j >= ROWS_RING:
                        pool.wait_ge(rows_doubled, c * F + (j - ROWS_RING + 1))
                        pool.sem_inc(pool_passed, 1)
                    for t in range(TILES):
                        pool.indirect_dma_start(rows[:, j % ROWS_RING, t, :], None, tables[j],
                                                bass.IndirectOffsetOnAxis(ap=idx[:, t, j:j + 1], axis=0)
                                                ).then_inc(rows_landed[j % ROWS_RING], 16)

            gather(0, True)
            with pool.Fori(1, CHUNKS) as c:
                gather(c, False)

        @block.sync
        def _(sp):
            for p in range(PIECES):
                stage, uses = stage_of(p)
                if uses > 1:
                    sp.wait_ge(kernel_split, p + 1 - (STAGES if p < EARLY else LATE_STAGES))
                for half in range(2):
                    sp.dma_start(loaded(p, half * E, half * E + E), pair_kernel[p]).then_inc(kernel_landed[stage], 16)
            for q in range(4):
                sp.dma_start(z_dram[Z_BANKS - 1, q * 32 + SUM_ROWS:q * 32 + 32, :],
                             dense[q * 4:q * 4 + 4, :]).then_inc(dense_placed, 16)

            def spill(c, kb):
                sp.wait_ge(bank_copied, c * Z_BANKS + kb + 1)
                if kb < Z_BANKS - 1:
                    sp.dma_start(z_dram[kb, :, bass.ds(c * N, N)], sums[:]).then_inc(bank_spilled, 16)
                else:
                    for q in range(4):
                        sp.dma_start(z_dram[kb, q * 32:q * 32 + SUM_ROWS, bass.ds(c * N, N)],
                                     sums[q * 32:q * 32 + SUM_ROWS, :]).then_inc(bank_spilled, 16)

            for kb in range(Z_BANKS - 1):
                spill(0, kb)
            with sp.Fori(1, CHUNKS) as c:
                spill(c - 1, Z_BANKS - 1)
                for kb in range(Z_BANKS - 1):
                    spill(c, kb)

            sp.wait_ge(duo_ready, (CHUNKS - 1) * DUOS + freed_duo)
            for dst, src in ((w1_sb, w1), (w2_sb, w2), (w3_sb, w3), (b1_sb, b1), (b2_sb, b2)):
                sp.dma_start(dst[:], src).then_inc(weights_landed, 16)
            sp.wait_ge(dense_placed, 4 * 16)
            for c in range(CHUNKS):
                if c == CHUNKS - 1:
                    spill(c, Z_BANKS - 1)
                sp.wait_ge(bank_spilled, (c + 1) * SPILLED)
                sp.dma_start(z_sb[:, c], z_dram[:, :, c * N:c * N + N].rearrange("k p n -> p k n")).then_inc(z_landed[c], 16)
            sp.wait_ge(y_kept, CHUNKS)
            sp.dma_start(out, y_sb[:]).then_inc(out_written, 16)
            sp.wait_ge(out_written, 16)

        @block.tensor
        def _(pe):
            def turn(c, j, first):
                pe.wait_ge(rows_doubled, c * F + j + 1)
                if j == 2:
                    pe.wait_ge(field_stored, c * F + 1)
                elif j > 2:
                    pe.wait_ge(field_split, c * (F - 1) + j - 2)
                elif not first:
                    pe.wait_ge(field_split, c * (F - 1) + j - 1)
                for t in range(TILES):
                    last = nc.tensor.transpose(turned[j % 2][:, t * P:(t + 1) * P],
                                               doubled[:, t].rearrange("p d e -> p (d e)"),
                                               identity[:])
                last.then_inc(field_turned, 1)

            def bilinear(c, d, first):
                if not first or d >= 2:
                    pe.wait_ge(duo_multiplied, c * DUOS + d - 1)
                for bank, group in enumerate(DUO[d]):
                    kind, j, k = group
                    if kind == "pair":
                        r = REGULAR.index(group)
                        parts = [(k_reg[:, r, :], j)]
                    else:
                        blocks = k_left[:, k].rearrange("p b e -> p (b e)")
                        parts = [(blocks[:, 0:2 * E], 4 * k + 1), (blocks[:, E:3 * E], 4 * k + 3)]
                    for n, (stationary, field) in enumerate(parts):
                        for half in range(2):
                            last = nc.tensor.matmul(y_ps[d % 2][:, bank, :], stationary,
                                                    halves[:, field % HALF_RING, half, :],
                                                    start=(n == 0 and half == 0),
                                                    stop=(n == len(parts) - 1 and half == 1))
                last.then_inc(duo_ready, 1)

            def add_up(c, quad, first):
                pe.wait_ge(duo_multiplied, c * DUOS + 2 * quad + 2)
                kb, s = quad // Z_QUADS, quad % Z_QUADS
                if s == 0 and not (first and kb < 2):
                    pe.wait_ge(bank_copied, c * Z_BANKS + kb - 1)
                for q in range(4):
                    last = nc.tensor.matmul(sum_ps[kb % 2][32 * q:32 * q + 32, :], selector[:, 30 - 2 * s:62 - 2 * s],
                                            products[:, (2 * quad + q // 2) % 4, q % 2, :],
                                            start=(s == 0), stop=(s == Z_QUADS - 1 or quad == QUADS - 1))
                last.then_inc(quad_summed, 1)

            def chunk(c, first):
                if first:
                    pe.wait_ge(identity_made, 1)
                    turn(c, 0, first)
                    turn(c, 1, first)
                    turn(c, 2, first)
                    turn(c, 3, first)
                    pe.wait_ge(zeros_made, 1)
                    pe.wait_ge(selector_made, 2)
                else:
                    add_up(c - 1, QUADS - 1, False)
                pieces = 0
                for d in range(DUOS):
                    if d in NEXT_TURN and first:
                        turn(c + 1, NEXT_TURN[d], False)
                    elif d in NEXT_TURN:
                        with pe.If(c < CHUNKS - 1):
                            turn(c + 1, NEXT_TURN[d], False)
                    for j in range(2, F):
                        if FIRST_DUO[j] == d:
                            if j + 2 < F:
                                turn(c, j + 2, first)
                            pe.wait_ge(field_split, c * (F - 1) + j)
                    if first and max(map(kernel_piece, DUO[d])) + 1 > pieces:
                        pieces = max(map(kernel_piece, DUO[d])) + 1
                        pe.wait_ge(kernel_split, pieces)
                    bilinear(c, d, first)
                    if d % 2 and d > 2:
                        add_up(c, d // 2 - 1, first)

            chunk(0, True)
            with pe.Fori(1, CHUNKS) as c:
                chunk(c, False)
            add_up(CHUNKS - 1, QUADS - 1, False)

            def layer1(c):
                pe.wait_ge(z_landed[c], 16)
                for n in range(4):
                    if c:
                        pe.wait_ge(h1_kept, (c - 1) * 4 + n + 1)
                    else:
                        pe.wait_ge(duo_multiplied, CHUNKS * DUOS)
                    for kb in range(4):
                        last = nc.tensor.matmul(y_ps[n // 2][:, n % 2, :], w1_sb[:, kb, n * P:n * P + P],
                                                z_sb[:, c, kb, :], start=(kb == 0), stop=(kb == 3))
                    last.then_inc(h1_ready, 1)

            def layer2(c):
                pe.wait_ge(h1_kept, 4 * c + 4)
                for n in range(2):
                    if c:
                        pe.wait_ge(h2_kept, (c - 1) * 2 + n + 1)
                    else:
                        pe.wait_ge(bank_copied, CHUNKS * Z_BANKS)
                    for kb in range(4):
                        last = nc.tensor.matmul(sum_ps[n][:], w2_sb[:, kb, n * P:n * P + P], h1_sb[:, c % 2, kb, :],
                                                start=(kb == 0), stop=(kb == 3))
                    last.then_inc(h2_ready, 1)

            def layer3(c):
                pe.wait_ge(h2_kept, 2 * c + 2)
                if c >= 2:
                    pe.wait_ge(y_kept, c - 1)
                for kb in range(2):
                    last = nc.tensor.matmul(turned[c % 2][0:1, :], w3_sb[:, kb:kb + 1], h2_sb[:, c % 2, kb, :],
                                            start=(kb == 0), stop=(kb == 1))
                last.then_inc(y_ready, 1)

            pe.wait_ge(weights_landed, 5 * 16)
            for step in range(CHUNKS + 2):
                if step < CHUNKS:
                    layer1(step)
                if 1 <= step <= CHUNKS:
                    layer2(step - 1)
                if step >= 2:
                    layer3(step - 2)

        @block.scalar
        def _(act):
            def as_groups(ap):
                return ap.rearrange("p (g b e) -> p g b e", b=2, e=E)

            def kernel_piece_high(p):
                stage, uses = stage_of(p)
                act.wait_ge(kernel_landed[stage], uses * 32)
                if p >= EARLY:
                    act.wait_ge(kernel_split, EARLY)
                nc.scalar.activation(kept(p, 0, P), as_groups(loaded(p, 0, P)), ACT.Copy).then_inc(kernel_high, 1)

            def double(c, j):
                act.wait_ge(rows_landed[j % ROWS_RING], (c * (F // ROWS_RING) + j // ROWS_RING + 1) * TILES * 16)
                if not isinstance(c, int) or j:
                    act.wait_ge(field_turned, c * F + j)
                nc.scalar.activation(doubled[:], rows[:, j % ROWS_RING].unsqueeze(2).broadcast_to([P, TILES, 2, E]),
                                     ACT.Copy).then_inc(rows_doubled, 1)

            def store(c, j, first):
                act.wait_ge(field_turned, c * F + j + 1)
                bank = turned[j % 2]
                ops = []
                if j:
                    if j > HALF_RING:
                        act.wait_ge(duo_ready, c * DUOS + LAST_MOVING[j - HALF_RING] + 1)
                    elif not first:
                        before = j + F - HALF_RING if j < HALF_RING else F - HALF_RING
                        act.wait_ge(duo_ready, (c - 1) * DUOS + LAST_MOVING[before] + 1)
                    last = nc.scalar.activation(halves[:, j % HALF_RING, 0, :], bank[:], ACT.Copy)
                if j < 2 * X_SLOTS:
                    if not first:
                        act.wait_ge(duo_multiplied, (c - 1) * DUOS + LAST_READ[j // 2] + 1)
                    elif j == FIRST_BORROWED_FIELD:
                        act.wait_ge(kernel_split, PIECES)
                    at = j % 2 * E
                    last = nc.scalar.activation(multiplier[at:at + E, j // 2, :], bank[at:at + E, :], ACT.Copy)
                if j % 4 == 2:
                    m = j // 4
                    if m:
                        act.wait_ge(duo_multiplied, c * DUOS + LEFT_DUO[m - 1] + 1)
                    elif not first:
                        act.wait_ge(duo_multiplied, (c - 1) * DUOS + LEFT_DUO[LEFT - 1] + 1)
                    act.wait_ge(field_stored, c * F + j - 1)
                    nc.scalar.activation(multiplier[0:E, L_SLOT, :], multiplier[0:E, j // 2 - 1, :], ACT.Copy)
                    last = nc.scalar.activation(multiplier[E:P, L_SLOT, :], bank[E:P, :], ACT.Copy)
                last.then_inc(field_stored, 1)

            def copy_bank(c, kb, first):
                act.wait_ge(quad_summed, c * QUADS + min(Z_QUADS * (kb + 1), QUADS))
                if not first or kb:
                    act.wait_ge(bank_spilled, c * SPILLED + kb * 16)
                nc.scalar.activation(sums[:], sum_ps[kb % 2][:], ACT.Copy).then_inc(bank_copied, 1)

            def chunk(c, first):
                double(c, 0)
                for j in range(F):
                    if first:
                        for p in range(PIECES_BY[j - 1] if j else 0, PIECES_BY[j]):
                            kernel_piece_high(p)
                    for kb in range(Z_BANKS - 1):
                        if COPY_BEFORE[kb] == j:
                            copy_bank(c, kb, first)
                    if not first and j + 1 < F:
                        double(c, j + 1)
                    store(c, j, first)
                    if first and j + 1 < F:
                        double(c, j + 1)
                    if j == 8 and not first:
                        copy_bank(c - 1, Z_BANKS - 1, False)
                for kb in range(Z_BANKS - 1):
                    if COPY_BEFORE[kb] >= F:
                        copy_bank(c, kb, first)

            chunk(0, True)
            with act.Fori(1, CHUNKS) as c:
                chunk(c, False)
            copy_bank(CHUNKS - 1, Z_BANKS - 1, False)

            def keep1(c):
                if c >= 2:
                    act.wait_ge(h2_ready, 2 * (c - 1))
                for n in range(4):
                    act.wait_ge(h1_ready, 4 * c + n + 1)
                    nc.scalar.activation(h1_sb[:, c % 2, n, :], y_ps[n // 2][:, n % 2, :], ACT.Relu,
                                         bias=b1_sb[:, n:n + 1]).then_inc(h1_kept, 1)

            def keep2(c):
                if c >= 2:
                    act.wait_ge(y_ready, c - 1)
                for n in range(2):
                    act.wait_ge(h2_ready, 2 * c + n + 1)
                    nc.scalar.activation(h2_sb[:, c % 2, n, :], sum_ps[n][:], ACT.Relu,
                                         bias=b2_sb[:, n:n + 1]).then_inc(h2_kept, 1)

            act.wait_ge(weights_landed, 5 * 16)
            for step in range(CHUNKS + 1):
                if step < CHUNKS:
                    keep1(step)
                if step >= 1:
                    keep2(step - 1)

        @block.vector
        def _(dve):
            nc.vector.memset(k_left[:, :, 1, :].bitcast(F32), 0.0).then_inc(zeros_made, 1)
            nc.vector.memset(selector[:], 0.0).then_inc(selector_cleared, 1)
            dve.wait_ge(selector_cleared, 1)
            nc.vector.memset(selector[0:E, 30:31], 1.0).then_inc(selector_made, 1)
            nc.vector.memset(selector[E:P, 31:32], 1.0).then_inc(selector_made, 1)

            def kernel_piece_low(p):
                dve.wait_ge(kernel_high, p + 1)
                nc.vector.tensor_tensor(kept(p, E, P), loaded(p, E, P).rearrange("p (g b e) -> p g b e", b=2, e=E),
                                        kept(p, E, P).bitcast(F32), ALU.subtract).then_inc(kernel_split, 1)

            def split(c, j):
                dve.wait_ge(field_stored, c * F + j + 1)
                nc.vector.tensor_tensor(halves[:, j % HALF_RING, 1, :], turned[j % 2][:],
                                        halves[:, j % HALF_RING, 0, :].bitcast(F32), ALU.subtract).then_inc(field_split, 1)

            def multiply(c, d, first):
                if not first or d >= 4:
                    dve.wait_ge(quad_summed, c * QUADS + d // 2 - 1)
                dve.wait_ge(duo_ready, c * DUOS + d + 1)
                s0, s1 = (slot_of(g) for g in DUO[d])
                if s0 == s1:
                    for bank in range(2):
                        last = nc.vector.tensor_tensor(products[:, d % 4, bank, :], y_ps[d % 2][:, bank, :],
                                                       multiplier[:, s0, :], ALU.mult)
                else:
                    last = nc.vector.tensor_tensor(products[:, d % 4], y_ps[d % 2][:],
                                                   multiplier[:, s0:s1 + 1:s1 - s0, :], ALU.mult)
                last.then_inc(duo_multiplied, 1)

            def chunk(c, first):
                def split_next(j):
                    if first:
                        for p in range(PIECES_BY[j - 1] if j > 1 else 0, PIECES_BY[j]):
                            kernel_piece_low(p)
                    split(c, j)

                for j in range(1 if first else 2, 4):
                    split_next(j)
                for d in range(DUOS):
                    if d in NEXT_SPLIT and first:
                        split(c + 1, NEXT_SPLIT[d])
                    elif d in NEXT_SPLIT:
                        with dve.If(c < CHUNKS - 1):
                            split(c + 1, NEXT_SPLIT[d])
                    for j in range(4, F):
                        if SPLIT_BEFORE[j] == d:
                            split_next(j)
                    for j in range(2, F):
                        if FIRST_DUO[j] == d:
                            dve.wait_ge(field_stored, c * F + j)
                    multiply(c, d, first)

            chunk(0, True)
            with dve.Fori(1, CHUNKS) as c:
                chunk(c, False)

            for c in range(CHUNKS):
                dve.wait_ge(y_ready, c + 1)
                nc.vector.tensor_copy(y_sb[:, c * N:c * N + N], turned[c % 2][0:1, :]).then_inc(y_kept, 1)


def kernel(**inputs):
    import numpy as np
    import concourse.bacc as bacc
    from concourse.bass_utils import run_bass_kernel_spmd

    pair_number = {}
    for i in range(F):
        for j in range(i + 1, F):
            pair_number[i, j] = len(pair_number)

    ids = np.ascontiguousarray(np.asarray(inputs["ids"]).reshape(CHUNKS, TILES, P, F).transpose(2, 0, 1, 3))
    order = [pair_number[p] for g in sorted(GROUPS, key=lambda g: g[0] != "left") for p in field_pairs(g)]
    k = np.asarray(inputs["L0_rec_kernel"])[:, order, :].reshape(E, PIECES, PIECE)
    pair_kernel = np.ascontiguousarray(k.transpose(1, 0, 2))
    pairs = len(pair_number)
    w1_rows = [pair_number[r] if isinstance(r, tuple) else pairs + r for r in z_rows()]
    w1 = np.ascontiguousarray(np.asarray(inputs["W_top1"])[w1_rows].reshape(4, P, H1).transpose(1, 0, 2))
    w2 = np.ascontiguousarray(np.asarray(inputs["W_top2"]).reshape(4, P, H2).transpose(1, 0, 2))
    w3 = np.ascontiguousarray(np.asarray(inputs["W_top3"]).reshape(2, P).T)
    b1 = np.ascontiguousarray(np.asarray(inputs["b_top1"]).reshape(4, P).T)
    b2 = np.ascontiguousarray(np.asarray(inputs["b_top2"]).reshape(2, P).T)
    dense = np.ascontiguousarray(np.asarray(inputs["dense_ctx"]).T)

    arrays = {"ids": ids, "pair_kernel": pair_kernel, "dense": dense, "w1": w1, "b1": b1, "w2": w2, "b2": b2, "w3": w3}
    for f in range(F):
        arrays[f"tbl_{f}"] = np.ascontiguousarray(inputs[f"tbl_{f}"])

    nc = bacc.Bacc("TRN2", target_bir_lowering=False, num_devices=1)
    ap = {n: nc.dram_tensor(n + "_dram", a.shape, mybir.dt.from_np(a.dtype), kind="ExternalInput").ap()
          for n, a in arrays.items()}
    z_dram = nc.dram_tensor("z_dram", (Z_BANKS, P, B), F32, kind="Internal").ap()
    out = nc.dram_tensor("out_dram", (1, B), F32, kind="ExternalOutput").ap()
    dlrm_tower(nc, ap["ids"], [ap[f"tbl_{f}"] for f in range(F)], ap["pair_kernel"], ap["dense"], ap["w1"], ap["b1"],
               ap["w2"], ap["b2"], ap["w3"], z_dram, out)
    r = run_bass_kernel_spmd(nc, [{n + "_dram": a for n, a in arrays.items()}], core_ids=[0])
    return r.results[0]["out_dram"].reshape(B, 1)
```

```python
from contextlib import ExitStack

import concourse.bass as bass
from concourse import mybir

F32 = mybir.dt.float32
F32R = mybir.dt.float32r
I32 = mybir.dt.int32
ALU = mybir.AluOpType
ACT = mybir.ActivationFunctionType

B, F, E = 2048, 32, 64
DENSE, H1, H2 = 16, 512, 256
P = 128
N = 512
CHUNKS = B // N
TILES = N // P

PAIRS = F // 2
AC_SLOT, AD_SLOT = PAIRS, PAIRS + 1
FOURS = F // 4
SLOTS = PAIRS + 2


KEPT = 8
EARLY_LAST = 5


def group_list():
    special = {m: [(4 * m + 1, AC_SLOT, m), (4 * m + 2, AD_SLOT, m)] for m in range(FOURS)}
    ac, ad = special[0]
    groups = [ac, ad, (3, 0, None), (2, 2, None), (2, 3, None), (3, 2, None), (3, 3, None)]
    ac, ad = special[1]
    groups += [(4, 0, None), (4, 4, None), (5, 0, None), (5, 4, None), ac]
    groups += [ad, (6, 0, None), (6, 4, None), (7, 0, None), (7, 2, None), (7, 4, None)]
    groups += [(j, k, None) for j in (8, 9) for k in (0, 1)]
    for j in range(10, F):
        if j % 4 == 2:
            groups += [(j, k, None) for k in range(2)] + special[j // 4]
            groups += [(j, k, None) for k in range(2, j // 2 - 1)]
        else:
            groups += [(j, k, None) for k in range(j // 2)]
    kept = [(F - 5, k, None) for k in range(PAIRS - 3 - KEPT, PAIRS - 3)]
    groups = [g for g in groups if g not in kept]
    groups.remove(special[FOURS - 1][0])
    at = groups.index((F - 2, 0, None))
    groups[at:at] = [special[FOURS - 1][0]] + kept
    soon = [(F - 1, k, None) for k in range(4)]
    groups = [g for g in groups if g not in soon]
    at = groups.index((F - 2, EARLY_LAST, None))
    return groups[:at] + soon + groups[at:]


def slot_of(group):
    return group[1]


def field_pairs(group):
    j, s, m = group
    if m is None:
        return (2 * s, j), (2 * s + 1, j)
    return (4 * m, j), (4 * m + (2 if s == AC_SLOT else 3), j)


GROUPS = group_list()
DUOS = len(GROUPS) // 2
QUADS = len(GROUPS) // 4
DUO = [sorted(GROUPS[2 * d:2 * d + 2], key=slot_of) for d in range(DUOS)]

Z_QUADS = P // 8
Z_BANKS = -(-QUADS // Z_QUADS)
SUM_ROWS = 2 * (QUADS - (Z_BANKS - 1) * Z_QUADS)

PIECE = 1024
PIECE_GROUPS = PIECE // (2 * E)
PIECES = len(GROUPS) // PIECE_GROUPS
STAGES, LATE_STAGES = 4, 2
EARLY = PIECES - STAGES
BORROWED_SLOT = PAIRS - LATE_STAGES * PIECE // N

ROW_RING = 4
HALF_RING = 4


def half_slots():
    slots = {}
    for j in range(1, F):
        if j % 4 >= 2 and j < F - 2:
            slots[j] = j % 4 - 2
        elif j < 20:
            slots[j] = 3 - j % 4
        else:
            slots[j] = 2 + j % 2
    return slots


HALF_SLOT = half_slots()


def predecessor(j):
    here = [i for i in range(1, j) if HALF_SLOT[i] == HALF_SLOT[j]]
    if here:
        return here[-1], 0
    return [i for i in range(1, F) if HALF_SLOT[i] == HALF_SLOT[j]][-1], 1


def stage_of(p):
    if p < EARLY:
        return p % STAGES, p // STAGES + 1
    return STAGES + (p - EARLY) % LATE_STAGES, (p - EARLY) // LATE_STAGES + 1


def duos_where(test):
    return [d for d in range(DUOS) if any(test(g) for g in DUO[d])]


FIRST_MOVING = {j: duos_where(lambda g: g[0] == j)[0] for j in range(1, F)}
LAST_MOVING = {j: duos_where(lambda g: g[0] == j)[-1] for j in range(1, F)}
LAST_READ = {s: duos_where(lambda g: g[1] == s or g[2] == s // 2)[-1] for s in range(PAIRS)}
SPECIAL_DUO = {m: duos_where(lambda g: g[2] == m)[-1] for m in range(FOURS)}
TOGETHER = 4
LENT = (4,)
STEPS = [(2, 3), (1,)] + [(2 * q, 2 * q + 1) for q in range(2, PAIRS)]
RANK = {j: r + 1 for r, j in enumerate(j for step in STEPS for j in step)}
FIRST_USE = {q: duos_where(lambda g: g[0] // 2 == q or (g[1] if g[2] is None else 2 * g[2] + 1) == q)[0]
             for q in range(PAIRS)}
FIRST_DUO = {q: min(FIRST_MOVING[2 * q], FIRST_MOVING[2 * q + 1]) for q in range(2, PAIRS)}
FIRST_DUO[PAIRS - 1] = FIRST_MOVING[F - 2]


def split_schedule():
    at = {}
    for q in range(2, PAIRS):
        free = max([0] + [LAST_MOVING[i] + 1 for i, last_chunk in map(predecessor, (2 * q, 2 * q + 1))
                          if not last_chunk])
        even = free + 1 + (free + 1) % 2
        first = FIRST_DUO[q]
        at[2 * q] = even if even < first else max(min(free, first), min(even, first - 1))
        at[2 * q + 1] = max(at[2 * q], min(at[2 * q] + 2, FIRST_MOVING[2 * q + 1] - 1))
        if q <= 6:
            for j in (2 * q, 2 * q + 1):
                at[j] = max(LAST_MOVING[predecessor(j)[0]] + 1, FIRST_DUO[q] - 3 + j % 2) if q > 2 else 1
    return at


SPLIT_BEFORE = split_schedule()
TURN_BEFORE = {q: FIRST_DUO[q - 3] if q > 5 else q - 4 for q in range(4, PAIRS)}
FIRST_TURN = {2: 1, 3: 2} | {q: FIRST_DUO[q - 2] if q in LENT else min(FIRST_USE[q] - 3, SPLIT_BEFORE[2 * q] - 2)
              for q in range(4, PAIRS)}
NEXT_LATE = {LAST_READ[0] + 3: 2, LAST_READ[0] + 4: 3}
FIRST_NEXT_TURN = {FIRST_TURN[PAIRS - 1] + 1: 0, FIRST_TURN[PAIRS - 1] + 2: 1, **NEXT_LATE}
NEXT_TURN = {FIRST_DUO[PAIRS - 3]: 0, FIRST_DUO[PAIRS - 2]: 1, **NEXT_LATE}
NEXT_SPLIT = {LAST_READ[0] + 4: 2, LAST_READ[0] + 6: 3, LAST_MOVING[F - 2] + 3: 1}

STARTING = [8, 14, 20, 20]
SECOND = 22
LAST_PIECES = BORROWED_SLOT - 1
PIECES_BY = {q: min(PIECES, SECOND - (SECOND - PIECES) * (q - 2) // (LAST_PIECES - 2)) for q in range(2, PAIRS)}


def piece_schedule():
    at = {p: min((p - STARTING[1]) // 4, 1) for p in range(STARTING[1], SECOND)}
    for q in range(3, PAIRS):
        start, end = SPLIT_BEFORE[2 * q - 1] + 2, SPLIT_BEFORE[2 * q + 1] + 2
        pieces = range(PIECES_BY[q - 1], PIECES_BY[q])
        for n, p in enumerate(pieces):
            at[p] = start + n * (end - start) // len(pieces)
    return at


PIECE_BEFORE = piece_schedule()
COPY_BEFORE = {kb: DUO[2 * (Z_QUADS * (kb + 1) + 1)][-1][0] // 2 + 2 for kb in range(Z_BANKS - 1)}
SPILL_BEFORE = {kb: -(-COPY_BEFORE[kb] // 2) for kb in range(Z_BANKS - 2)}


def z_rows():
    rows, dense = [], 0
    for kb in range(Z_BANKS):
        for r in range(P):
            column_tile, s, half = r // 32, r % 32 // 2, r % 2
            quad = kb * Z_QUADS + s
            if quad < QUADS:
                group = DUO[2 * quad + column_tile // 2][column_tile % 2]
                rows.append(field_pairs(group)[half])
            else:
                rows.append(dense)
                dense += 1
    return rows


def dlrm_tower(nc, ids, tables, pair_kernel, dense, w1, b1, w2, b2, w3, z_dram, out):
    with ExitStack() as ctx:
        def psum(name, shape):
            return ctx.enter_context(nc.psum_tensor(name, shape, F32))

        def sem(name):
            return ctx.enter_context(nc.semaphore(name))

        place = [-(-nc.sbuf_base // 32) * 32]

        def sb(name, shape, dt, at=place):
            width = 4
            for s in shape[1:]:
                width *= s
            t = nc.alloc_sbuf_tensor_at(name, shape, dt, offset=at[0])
            at[0] += -(-width // 32) * 32
            return t

        kernel_at = place[0]
        freed = [place[0]]
        kernel_sb = sb("kernel_sb", [P, len(GROUPS), 2 * E], F32R)
        staged = [nc.alloc_sbuf_tensor_at(f"staged{i}", [P, PIECE], F32, offset=kernel_at + (EARLY + i) * 4 * PIECE)
                  for i in range(STAGES)]
        multiplier = sb("multiplier", [P, SLOTS, N], F32)
        rows = sb("rows", [P, ROW_RING, TILES, 2, E], F32)
        halves = sb("halves", [P, HALF_RING, 2, N], F32R)
        products = sb("products", [P, 4, 2, N], F32)
        sums = sb("sums", [P, N], F32)
        idx = sb("idx", [P, TILES, F], I32)
        identity = sb("identity", [P, P], F32)
        selector = sb("selector", [P, 62], F32)
        w1_sb = sb("w1_sb", [P, 4, H1], F32, freed)
        w2_sb = sb("w2_sb", [P, 4, H2], F32, freed)
        w3_sb = sb("w3_sb", [P, 2, 32], F32, freed)
        b1_sb = sb("b1_sb", [P, 4], F32, freed)
        b2_sb = sb("b2_sb", [P, 2], F32, freed)
        z_sb = sb("z_sb", [P, CHUNKS, Z_BANKS, N], F32, freed)
        h1_sb = sb("h1_sb", [P, 2, 4, N], F32, freed)
        h2_sb = sb("h2_sb", [P, CHUNKS, 2, N], F32, freed)
        y_sb = sb("y_sb", [P, N], F32, freed)
        freed_duo = -(-(freed[0] - kernel_at) // (4 * 2 * E * 2))

        y_ps = [psum(f"y_ps{i}", [P, 2, N]) for i in range(2)]
        sum_ps = [psum(f"sum_ps{i}", [P, N]) for i in range(2)]
        turned = [psum(f"turned{i}", [P, N]) for i in range(2)]

        ids_landed = sem("ids_landed")
        rows_landed = [sem(f"rows_landed{i}") for i in range(ROW_RING)]
        pool_passed = sem("pool_passed")
        sync_passed = sem("sync_passed")
        identity_cleared = sem("identity_cleared")
        identity_made = sem("identity_made")
        selector_cleared = sem("selector_cleared")
        selector_made = sem("selector_made")
        kernel_landed = [sem(f"kernel_landed{i}") for i in range(STAGES + LATE_STAGES)]
        kernel_high = sem("kernel_high")
        kernel_split = sem("kernel_split")
        pair_turned = sem("pair_turned")
        pair_stored = sem("pair_stored")
        special_stored = sem("special_stored")
        field_high = sem("field_high")
        field_split = sem("field_split")
        field_ready = sem("field_ready")
        field_moved = sem("field_moved")
        duo_ready = sem("duo_ready")
        duo_multiplied = sem("duo_multiplied")
        quad_summed = sem("quad_summed")
        bank_copied = sem("bank_copied")
        bank_spilled = sem("bank_spilled")
        dense_placed = sem("dense_placed")
        weights_landed = sem("weights_landed")
        z_landed = [sem(f"z_landed{c}") for c in range(CHUNKS)]
        h1_ready = sem("h1_ready")
        h1_kept = sem("h1_kept")
        h2_ready = sem("h2_ready")
        h2_kept = sem("h2_kept")
        y_ready = sem("y_ready")
        y_kept = sem("y_kept")
        out_written = sem("out_written")

        SPILLED = (Z_BANKS - 1 + 4) * 16

        def loaded(p, lo, hi):
            stage = stage_of(p)[0]
            if stage < STAGES:
                return staged[stage][lo:hi, :]
            at = BORROWED_SLOT + (stage - STAGES) * PIECE // N
            return multiplier[lo:hi, at:at + PIECE // N, :].rearrange("p s n -> p (s n)")

        def kept(p, lo, hi):
            return kernel_sb[lo:hi, p * PIECE_GROUPS:(p + 1) * PIECE_GROUPS, :].rearrange("p g e -> p (g e)")

        block = ctx.enter_context(nc.Block())

        @block.gpsimd
        def _(pool):
            def make_identity():
                nc.gpsimd.memset(identity[:], 0.0).then_inc(identity_cleared, 1)
                pool.wait_ge(identity_cleared, 1)
                nc.gpsimd.affine_select(out=identity[:], in_=identity[:], compare_op=ALU.not_equal, fill=1.0, base=0,
                                        pattern=[[-1, P]], channel_multiplier=1).then_inc(identity_made, 1)

            def gather(c, first):
                if not first:
                    for s in range(ROW_RING):
                        pool.wait_ge(rows_landed[s], c * (PAIRS // ROW_RING) * 2 * TILES * 16)
                        pool.sem_inc(pool_passed, 1)
                src = ids[:, 0] if first else ids[:, bass.ds(c, 1)].rearrange("p o t f -> p (o t) f")
                pool.dma_start(idx[:], src).then_inc(ids_landed, 16)
                if first:
                    make_identity()
                pool.wait_ge(ids_landed, c * 16 + 16)
                pool.sem_inc(pool_passed, 1)
                for q in range(PAIRS):
                    if not first or q >= ROW_RING:
                        pool.wait_ge(pair_turned, c * PAIRS + (q - ROW_RING + 1))
                        pool.sem_inc(pool_passed, 1)
                    for h in range(2):
                        j = 2 * q + h
                        for t in range(TILES):
                            pool.indirect_dma_start(rows[:, q % ROW_RING, t, h, :], None, tables[j],
                                                    bass.IndirectOffsetOnAxis(ap=idx[:, t, j:j + 1], axis=0)
                                                    ).then_inc(rows_landed[q % ROW_RING], 16)

            gather(0, True)
            with pool.Fori(1, CHUNKS) as c:
                gather(c, False)

        @block.sync
        def _(sp):
            def load(p):
                stage, uses = stage_of(p)
                if uses > 1:
                    sp.wait_ge(kernel_split, p + 1 - (STAGES if p < EARLY else LATE_STAGES))
                for half in range(2):
                    sp.dma_start(loaded(p, half * E, half * E + E), pair_kernel[p]).then_inc(kernel_landed[stage], 16)

            def special(c, m, first):
                sp.wait_ge(pair_stored, c * PAIRS + 2 * m + 2)
                sp.sem_inc(sync_passed, 1)
                if m:
                    sp.wait_ge(duo_multiplied, c * DUOS + SPECIAL_DUO[m - 1] + 1)
                elif not first:
                    sp.wait_ge(duo_multiplied, (c - 1) * DUOS + SPECIAL_DUO[FOURS - 1] + 1)
                low, high = slice(0, E), slice(E, P)
                for slot, source in ((AC_SLOT, low), (AD_SLOT, high)):
                    sp.dma_start(multiplier[low, slot, :], multiplier[low, 2 * m, :]).then_inc(special_stored, 16)
                    sp.dma_start(multiplier[high, slot, :],
                                 multiplier[source, 2 * m + 1, :]).then_inc(special_stored, 16)

            def spill(c, kb):
                sp.wait_ge(bank_copied, c * Z_BANKS + kb + 1)
                if kb < Z_BANKS - 1:
                    sp.dma_start(z_dram[kb, :, bass.ds(c * N, N)], sums[:]).then_inc(bank_spilled, 16)
                else:
                    for q in range(4):
                        sp.dma_start(z_dram[kb, q * 32:q * 32 + SUM_ROWS, bass.ds(c * N, N)],
                                     sums[q * 32:q * 32 + SUM_ROWS, :]).then_inc(bank_spilled, 16)

            def chunk(c, first):
                loads = 0
                for m in range(FOURS):
                    if first:
                        for p in range(loads, PIECES_BY[2 * m + 1] if m else STARTING[1] + 2):
                            load(p)
                            loads = p + 1
                    for kb in range(Z_BANKS - 2):
                        if SPILL_BEFORE[kb] == m:
                            spill(c, kb)
                    special(c, m, first)
                    if m == 3 and not first:
                        spill(c - 1, Z_BANKS - 1)
                spill(c, Z_BANKS - 2)

            chunk(0, True)
            for q in range(4):
                sp.dma_start(z_dram[Z_BANKS - 1, q * 32 + SUM_ROWS:q * 32 + 32, :],
                             dense[q * 4:q * 4 + 4, :]).then_inc(dense_placed, 16)

            with sp.Fori(1, CHUNKS) as c:
                chunk(c, False)

            sp.wait_ge(duo_ready, (CHUNKS - 1) * DUOS + freed_duo)
            for dst, src in ((w1_sb, w1), (w2_sb, w2), (w3_sb, w3), (b1_sb, b1), (b2_sb, b2)):
                sp.dma_start(dst[:], src).then_inc(weights_landed, 16)
            sp.wait_ge(dense_placed, 4 * 16)
            for c in range(CHUNKS):
                if c == CHUNKS - 1:
                    spill(c, Z_BANKS - 1)
                sp.wait_ge(bank_spilled, (c + 1) * SPILLED)
                sp.dma_start(z_sb[:, c],
                             z_dram[:, :, c * N:c * N + N].rearrange("k p n -> p k n")).then_inc(z_landed[c], 16)
            sp.wait_ge(y_kept, 1)
            sp.dma_start(out.rearrange("o (c n) -> (o c) n", n=N), y_sb[0:P:32, :]).then_inc(out_written, 16)
            sp.wait_ge(out_written, 16)

        @block.tensor
        def _(pe):
            def turn(c, q, first):
                pe.wait_ge(rows_landed[q % ROW_RING], (c * (PAIRS // ROW_RING) + q // ROW_RING + 1) * 2 * TILES * 16)
                if q >= 2 or not first:
                    pe.wait_ge(pair_stored, c * PAIRS + q - 1)
                for t in range(TILES):
                    last = nc.tensor.transpose(turned[q % 2][:, t * P:(t + 1) * P],
                                               rows[:, q % ROW_RING, t].rearrange("p h e -> p (h e)"), identity[:])
                last.then_inc(pair_turned, 1)

            def bilinear(c, d, first):
                if not first or d >= 2:
                    pe.wait_ge(duo_multiplied, c * DUOS + d - 1)
                for bank, group in enumerate(DUO[d]):
                    for half in range(2):
                        last = nc.tensor.matmul(y_ps[d % 2][:, bank, :], kernel_sb[:, GROUPS.index(group), :],
                                                halves[:, HALF_SLOT[group[0]], half, :],
                                                start=(half == 0), stop=(half == 1))
                last.then_inc(duo_ready, 1)

            def add_up(c, quad, first):
                pe.wait_ge(duo_multiplied, c * DUOS + 2 * quad + 2)
                kb, s = quad // Z_QUADS, quad % Z_QUADS
                if s == 0 and not (first and kb < 2):
                    pe.wait_ge(bank_copied, c * Z_BANKS + kb - 1)
                for q in range(4):
                    last = nc.tensor.matmul(sum_ps[kb % 2][32 * q:32 * q + 32, :], selector[:, 30 - 2 * s:62 - 2 * s],
                                            products[:, (2 * quad + q // 2) % 4, q % 2, :],
                                            start=(s == 0), stop=(s == Z_QUADS - 1 or quad == QUADS - 1))
                last.then_inc(quad_summed, 1)

            def chunk(c, first):
                if first:
                    pe.wait_ge(identity_made, 1)
                    turn(c, 0, first)
                    turn(c, 1, first)
                pieces, fields = 0, 0
                for d in range(DUOS):
                    if d in FIRST_NEXT_TURN and first:
                        turn(c + 1, FIRST_NEXT_TURN[d], False)
                    elif d in NEXT_TURN and not first:
                        with pe.If(c < CHUNKS - 1):
                            turn(c + 1, NEXT_TURN[d], False)
                    for q, before in (FIRST_TURN if first else TURN_BEFORE).items():
                        if before == d:
                            turn(c, q, first)
                    if max(RANK[g[0]] for g in DUO[d]) > fields:
                        fields = max(RANK[g[0]] for g in DUO[d])
                        pe.wait_ge(field_ready, c * (F - 1) + fields)
                    if first and d * 2 // PIECE_GROUPS + 1 > pieces:
                        pieces = d * 2 // PIECE_GROUPS + 1
                        pe.wait_ge(kernel_split, pieces)
                    bilinear(c, d, first)
                    if d % 2 and d > 2:
                        add_up(c, d // 2 - 1, first)
                    elif d == 0 and not first:
                        add_up(c - 1, QUADS - 1, False)

            chunk(0, True)
            with pe.Fori(1, CHUNKS) as c:
                chunk(c, False)
            add_up(CHUNKS - 1, QUADS - 1, False)

            def layer1(c):
                pe.wait_ge(z_landed[c], 16)
                for n in range(4):
                    if c:
                        pe.wait_ge(h1_kept, (c - 1) * 4 + n + 1)
                    else:
                        pe.wait_ge(duo_multiplied, CHUNKS * DUOS)
                    for kb in range(4):
                        last = nc.tensor.matmul(y_ps[n // 2][:, n % 2, :], w1_sb[:, kb, n * P:n * P + P],
                                                z_sb[:, c, kb, :], start=(kb == 0), stop=(kb == 3))
                    last.then_inc(h1_ready, 1)

            def layer2(c):
                pe.wait_ge(h1_kept, 4 * c + 4)
                for n in range(2):
                    if c:
                        pe.wait_ge(h2_kept, (c - 1) * 2 + n + 1)
                    else:
                        pe.wait_ge(bank_copied, CHUNKS * Z_BANKS)
                    for kb in range(4):
                        last = nc.tensor.matmul(sum_ps[n][:], w2_sb[:, kb, n * P:n * P + P], h1_sb[:, c % 2, kb, :],
                                                start=(kb == 0), stop=(kb == 3))
                    last.then_inc(h2_ready, 1)

            def layer3():
                pe.wait_ge(h2_kept, 2 * CHUNKS)
                for kb in range(2):
                    for c in range(CHUNKS):
                        last = nc.tensor.matmul(turned[0][32 * c:32 * c + 32, :], w3_sb[:, kb, :], h2_sb[:, c, kb, :],
                                                start=(kb == 0), stop=(kb == 1))
                last.then_inc(y_ready, 1)

            pe.wait_ge(weights_landed, 5 * 16)
            for step in range(CHUNKS + 1):
                if step < CHUNKS:
                    layer1(step)
                if step >= 1:
                    layer2(step - 1)
            layer3()

        @block.scalar
        def _(act):
            def kernel_piece_high(p):
                stage, uses = stage_of(p)
                act.wait_ge(kernel_landed[stage], uses * 32)
                if p >= EARLY:
                    act.wait_ge(kernel_split, EARLY)
                nc.scalar.activation(kept(p, 0, P), loaded(p, 0, P), ACT.Copy).then_inc(kernel_high, 1)

            def copy(dst, src):
                return nc.scalar.activation(dst, src, ACT.Copy)

            def half(h):
                return slice(h * E, h * E + E)

            def store(c, q, first):
                act.wait_ge(pair_turned, c * PAIRS + q + 1)
                if not first:
                    act.wait_ge(duo_multiplied, (c - 1) * DUOS + LAST_READ[q] + 1)
                elif q == BORROWED_SLOT:
                    act.wait_ge(kernel_split, PIECES)
                copy(multiplier[:, q, :], turned[q % 2][:]).then_inc(pair_stored, 1)

            def prepare(c, fields, first):
                own = {j: half(j % 2) for j in fields}
                other = {j: half(1 - j % 2) for j in fields}
                for j in fields:
                    before, last_chunk = predecessor(j)
                    if not last_chunk:
                        act.wait_ge(duo_ready, c * DUOS + LAST_MOVING[before] + 1)
                    elif not first:
                        act.wait_ge(duo_ready, (c - 1) * DUOS + LAST_MOVING[before] + 1)
                    act.wait_ge(pair_stored, c * PAIRS + j // 2 + 1)
                    copy(halves[own[j], HALF_SLOT[j], 0, :], multiplier[own[j], j // 2, :]).then_inc(field_high, 1)
                for j in fields:
                    act.wait_ge(field_high, c * (F - 1) + RANK[j])
                    copy(halves[other[j], HALF_SLOT[j], 0, :], halves[own[j], HALF_SLOT[j], 0, :].bitcast(F32))
                    act.wait_ge(field_split, c * (F - 1) + RANK[j])
                    copy(halves[other[j], HALF_SLOT[j], 1, :],
                         halves[own[j], HALF_SLOT[j], 1, :].bitcast(F32)).then_inc(field_ready, 1)

            def prepare_pair(c, q, first):
                (e, o), (low, high) = (HALF_SLOT[2 * q], HALF_SLOT[2 * q + 1]), (half(0), half(1))
                act.wait_ge(duo_ready, c * DUOS + LAST_MOVING[predecessor(2 * q)[0]] + 1)
                act.wait_ge(pair_stored, c * PAIRS + q + 1)
                copy(halves[:, e, 0, :], multiplier[:, q, :]).then_inc(field_high, 2)
                act.wait_ge(duo_ready, c * DUOS + LAST_MOVING[predecessor(2 * q + 1)[0]] + 1)
                act.wait_ge(field_high, c * (F - 1) + RANK[2 * q + 1])
                for n in range(2):
                    if n == 1:
                        act.wait_ge(field_split, c * (F - 1) + RANK[2 * q + 1])
                    copy(halves[high, o, n, :], halves[high, e, n, :].bitcast(F32))
                    copy(halves[low, o, n, :], halves[high, e, n, :].bitcast(F32)).then_inc(field_moved, 1)
                act.wait_ge(field_moved, (c * (PAIRS - TOGETHER) + q - TOGETHER + 1) * 2)
                for n in range(2):
                    last = copy(halves[high, e, n, :], halves[low, e, n, :].bitcast(F32))
                last.then_inc(field_ready, 2)

            def copy_bank(c, kb, first):
                act.wait_ge(quad_summed, c * QUADS + min(Z_QUADS * (kb + 1), QUADS))
                if not first or kb:
                    act.wait_ge(bank_spilled, c * SPILLED + kb * 16)
                nc.scalar.activation(sums[:], sum_ps[kb % 2][:], ACT.Copy).then_inc(bank_copied, 1)

            def chunk(c, first):
                def starting(q):
                    if first:
                        for p in range(STARTING[q - 1] if q else 0, STARTING[q]):
                            kernel_piece_high(p)
                    store(c, q, first)

                starting(0)
                starting(1)
                prepare(c, (2, 3), first)
                if first:
                    prepare(c, (1,), first)
                starting(2)
                starting(3)
                if first:
                    for p in range(STARTING[-1], SECOND):
                        kernel_piece_high(p)
                else:
                    prepare(c, (1,), first)
                for q in range(2, PAIRS):
                    for kb in range(Z_BANKS - 1):
                        if COPY_BEFORE[kb] == q:
                            copy_bank(c, kb, first)
                    if first and q + 1 in LENT:
                        store(c, q + 1, first)
                    if q < TOGETHER:
                        prepare(c, (2 * q, 2 * q + 1), first)
                    else:
                        prepare_pair(c, q, first)
                    if first and q + 1 < PAIRS:
                        for p in range(PIECES_BY[q], PIECES_BY[q + 1]):
                            kernel_piece_high(p)
                    if not first and q + 2 < PAIRS:
                        store(c, q + 2, first)
                    if first and 3 < q + 1 < PAIRS and q + 1 not in LENT:
                        store(c, q + 1, first)
                    if q == 6 and not first:
                        copy_bank(c - 1, Z_BANKS - 1, False)
                for kb in range(Z_BANKS - 1):
                    if COPY_BEFORE[kb] >= PAIRS:
                        copy_bank(c, kb, first)

            chunk(0, True)
            with act.Fori(1, CHUNKS) as c:
                chunk(c, False)
            copy_bank(CHUNKS - 1, Z_BANKS - 1, False)

            def keep1(c):
                if c >= 2:
                    act.wait_ge(h2_ready, 2 * (c - 1))
                for n in range(4):
                    act.wait_ge(h1_ready, 4 * c + n + 1)
                    nc.scalar.activation(h1_sb[:, c % 2, n, :], y_ps[n // 2][:, n % 2, :], ACT.Relu,
                                         bias=b1_sb[:, n:n + 1]).then_inc(h1_kept, 1)

            def keep2(c):
                for n in range(2):
                    act.wait_ge(h2_ready, 2 * c + n + 1)
                    nc.scalar.activation(h2_sb[:, c, n, :], sum_ps[n][:], ACT.Relu,
                                         bias=b2_sb[:, n:n + 1]).then_inc(h2_kept, 1)

            act.wait_ge(weights_landed, 5 * 16)
            for step in range(CHUNKS + 1):
                if step < CHUNKS:
                    keep1(step)
                if step >= 1:
                    keep2(step - 1)

        @block.vector
        def _(dve):
            nc.vector.memset(selector[:], 0.0).then_inc(selector_cleared, 1)
            dve.wait_ge(selector_cleared, 1)
            nc.vector.memset(selector[0:E, 30:31], 1.0).then_inc(selector_made, 1)
            nc.vector.memset(selector[E:P, 31:32], 1.0).then_inc(selector_made, 1)

            def kernel_piece_low(p):
                dve.wait_ge(kernel_high, p + 1)
                nc.vector.tensor_tensor(kept(p, E, P), loaded(p, E, P), kept(p, E, P).bitcast(F32),
                                        ALU.subtract).then_inc(kernel_split, 1)

            def split(c, j):
                if j // 2 >= TOGETHER:
                    fields, at = 2, slice(0, P)
                else:
                    fields, at = 1, slice(j % 2 * E, j % 2 * E + E)
                dve.wait_ge(field_high, c * (F - 1) + RANK[j + fields - 1])
                nc.vector.tensor_tensor(halves[at, HALF_SLOT[j], 1, :], multiplier[at, j // 2, :],
                                        halves[at, HALF_SLOT[j], 0, :].bitcast(F32),
                                        ALU.subtract).then_inc(field_split, fields)

            def multiply(c, d, first):
                if not first or d >= 4:
                    dve.wait_ge(quad_summed, c * QUADS + d // 2 - 1)
                dve.wait_ge(duo_ready, c * DUOS + d + 1)
                s0, s1 = (slot_of(g) for g in DUO[d])
                if s0 == s1:
                    for bank in range(2):
                        last = nc.vector.tensor_tensor(products[:, d % 4, bank, :], y_ps[d % 2][:, bank, :],
                                                       multiplier[:, s0, :], ALU.mult)
                else:
                    last = nc.vector.tensor_tensor(products[:, d % 4], y_ps[d % 2][:],
                                                   multiplier[:, s0:s1 + 1:s1 - s0, :], ALU.mult)
                last.then_inc(duo_multiplied, 1)

            def chunk(c, first):
                if first:
                    for p in range(STARTING[1]):
                        kernel_piece_low(p)
                    for j in (2, 3, 1):
                        split(c, j)
                pairs, fours = 0, 0
                for d in range(DUOS):
                    if d in NEXT_SPLIT and first:
                        split(c + 1, NEXT_SPLIT[d])
                    elif d in NEXT_SPLIT:
                        with dve.If(c < CHUNKS - 1):
                            split(c + 1, NEXT_SPLIT[d])
                    for p in range(STARTING[1], PIECES):
                        if first and PIECE_BEFORE[p] == d:
                            kernel_piece_low(p)
                    for j in range(4, F):
                        if SPLIT_BEFORE[j] == d and (j < 2 * TOGETHER or j % 2 == 0):
                            split(c, j)
                    for _, s, m in DUO[d]:
                        if m is None and s + 1 > pairs:
                            pairs = s + 1
                            dve.wait_ge(pair_stored, c * PAIRS + pairs)
                        elif m is not None and m + 1 > fours:
                            fours = m + 1
                            dve.wait_ge(special_stored, (c * FOURS + fours) * 64)
                    multiply(c, d, first)

            chunk(0, True)
            with dve.Fori(1, CHUNKS) as c:
                chunk(c, False)

            dve.wait_ge(y_ready, 1)
            nc.vector.tensor_copy(y_sb[:], turned[0][:]).then_inc(y_kept, 1)


def kernel(**inputs):
    import numpy as np
    import concourse.bacc as bacc
    from concourse.bass_utils import run_bass_kernel_spmd

    pair_number = {}
    for i in range(F):
        for j in range(i + 1, F):
            pair_number[i, j] = len(pair_number)

    ids = np.ascontiguousarray(np.asarray(inputs["ids"]).reshape(CHUNKS, TILES, P, F).transpose(2, 0, 1, 3))
    by_pair = np.asarray(inputs["L0_rec_kernel"]).transpose(1, 0, 2)
    k = np.stack([by_pair[pair_number[i, j]] if i < j else by_pair[pair_number[j, i]].T
                  for g in GROUPS for i, j in field_pairs(g)], axis=1).reshape(E, PIECES, PIECE)
    pair_kernel = np.ascontiguousarray(k.transpose(1, 0, 2))
    pairs = len(pair_number)
    w1_rows = [pair_number[min(r), max(r)] if isinstance(r, tuple) else pairs + r for r in z_rows()]
    w1 = np.ascontiguousarray(np.asarray(inputs["W_top1"])[w1_rows].reshape(4, P, H1).transpose(1, 0, 2))
    w2 = np.ascontiguousarray(np.asarray(inputs["W_top2"]).reshape(4, P, H2).transpose(1, 0, 2))
    w3 = np.ascontiguousarray(np.broadcast_to(np.asarray(inputs["W_top3"]).reshape(2, P).T[:, :, None], (P, 2, 32)))
    b1 = np.ascontiguousarray(np.asarray(inputs["b_top1"]).reshape(4, P).T)
    b2 = np.ascontiguousarray(np.asarray(inputs["b_top2"]).reshape(2, P).T)
    dense = np.ascontiguousarray(np.asarray(inputs["dense_ctx"]).T)

    arrays = {"ids": ids, "pair_kernel": pair_kernel, "dense": dense, "w1": w1, "b1": b1, "w2": w2, "b2": b2, "w3": w3}
    for f in range(F):
        arrays[f"tbl_{f}"] = np.ascontiguousarray(inputs[f"tbl_{f}"])

    nc = bacc.Bacc("TRN2", target_bir_lowering=False, num_devices=1)
    ap = {n: nc.dram_tensor(n + "_dram", a.shape, mybir.dt.from_np(a.dtype), kind="ExternalInput").ap()
          for n, a in arrays.items()}
    z_dram = nc.dram_tensor("z_dram", (Z_BANKS, P, B), F32, kind="Internal").ap()
    out = nc.dram_tensor("out_dram", (1, B), F32, kind="ExternalOutput").ap()
    dlrm_tower(nc, ap["ids"], [ap[f"tbl_{f}"] for f in range(F)], ap["pair_kernel"], ap["dense"], ap["w1"], ap["b1"],
               ap["w2"], ap["b2"], ap["w3"], z_dram, out)
    r = run_bass_kernel_spmd(nc, [{n + "_dram": a for n, a in arrays.items()}], core_ids=[0])
    return r.results[0]["out_dram"].reshape(B, 1)
```
